# Optimizing a Trainium2 kernel written in Bass

```python
import numpy as np
import jax
import jax.numpy as jnp

def _softmax(x, axis=-1):
    return jax.nn.softmax(x, axis=axis)

def _gelu(x):
    return jax.nn.gelu(x, approximate=True)

def _silu(x):
    return jax.nn.silu(x)

def _sigmoid(x):
    return jax.nn.sigmoid(x)

def _layernorm(x, axis=-1, eps=1e-05):
    m = jnp.mean(x, axis=axis, keepdims=True)
    v = jnp.var(x, axis=axis, keepdims=True)
    return (x - m) / jnp.sqrt(v + eps)

def _scatter_add(tgt, idx, src, axis=0):
    return tgt.at[idx].add(src)

def _segment_sum(src, seg, n):
    return jax.ops.segment_sum(src, seg, n)
kernel_name = 'mk_audio_tower_d1_tok_audfeat1024_r4_504683'

def setup_inputs(seed: int=0):
    np.random.seed(seed)
    _w = jnp.asarray

    def _rec_inputs():
        import jax
        import jax.numpy as jnp
        _rk = jax.random.key(seed)
        x = -7.10856e-05 + 0.999911 * jax.random.normal(jax.random.fold_in(_rk, 1), (8, 750, 256), jnp.float32)
        return x
    x = _rec_inputs()

    def _L0_tok_setup():
        import jax, jax.numpy as jnp
        import numpy as np
        N_EMBD = 256
        RF = 2
        FAN_IN = N_EMBD * RF
        EPS = 1e-05
        key = jax.random.key(seed)
        kx, kw, kb = jax.random.split(key, 3)
        x = jax.random.normal(kx, (16, 1024, N_EMBD), dtype=jnp.float32)
        ln_gamma = jnp.ones((FAN_IN,), dtype=jnp.float32)
        ln_beta = jnp.zeros((FAN_IN,), dtype=jnp.float32)
        bound = 1.0 / np.sqrt(FAN_IN)
        W = jax.random.uniform(kw, (N_EMBD, FAN_IN), dtype=jnp.float32, minval=-bound, maxval=bound)
        b = jax.random.uniform(kb, (N_EMBD,), dtype=jnp.float32, minval=-bound, maxval=bound)
        return {'x': x, 'ln_gamma': ln_gamma, 'ln_beta': ln_beta, 'W': W, 'b': b}
    _L0_tok_all = _L0_tok_setup()
    _L0_tok_in = {k: v for k, v in _L0_tok_all.items() if k in ('ln_gamma', 'ln_beta', 'W', 'b')}
    del _L0_tok_all

    def _L0_attn_setup():
        import jax, jax.numpy as jnp
        import numpy as np
        D_MODEL = 256
        D_STATE = 32
        D_CONV = 4
        BATCH = 2
        SEQ = 512

        def _forward(x, W_in, W_out, conv_w, conv_b, A_log, D_param):
            B, L, D = x.shape
            N = A_log.shape[0]
            K = conv_w.shape[-1]
            proj = x @ W_in.T
            u, delta, BC = jnp.split(proj, 3, axis=-1)
            u_c = jnp.transpose(u, (0, 2, 1))
            u_c = jax.lax.conv_general_dilated(u_c, conv_w, window_strides=(1,), padding=[(K - 1, 0)], feature_group_count=D, dimension_numbers=('NCH', 'OIH', 'NCH'))
            u = jnp.transpose(u_c, (0, 2, 1)) + conv_b[None, None, :]
            delta = jax.nn.softplus(delta)
            A_T = -jnp.exp(A_log).T
            Bm = BC[..., :N]
            Cm = BC[..., N:2 * N]

            def step(h, xt):
                d_t, b_t, c_t, u_t = xt
                h = h * jnp.exp(d_t[:, :, None] * A_T[None]) + b_t[:, None, :] * u_t[:, :, None]
                y = jnp.einsum('bdn,bn->bd', h, c_t)
                return (h, y)
            h0 = jnp.zeros((B, D, N), x.dtype)
            xs = (jnp.swapaxes(delta, 0, 1), jnp.swapaxes(Bm, 0, 1), jnp.swapaxes(Cm, 0, 1), jnp.swapaxes(u, 0, 1))
            _, ys = jax.lax.scan(step, h0, xs)
            y = jnp.swapaxes(ys, 0, 1)
            out = (y + u * D_param[None, None, :]) @ W_out.T
            return out
        key = jax.random.key(seed)
        ks = jax.random.split(key, 7)
        x = jax.random.normal(ks[0], (BATCH, SEQ, D_MODEL), jnp.float32)
        W_in = jax.random.normal(ks[1], (3 * D_MODEL, D_MODEL), jnp.float32) / np.sqrt(D_MODEL).astype(np.float32)
        W_out = jax.random.normal(ks[2], (D_MODEL, D_MODEL), jnp.float32) / np.sqrt(D_MODEL).astype(np.float32)
        conv_w = jax.random.normal(ks[3], (D_MODEL, 1, D_CONV), jnp.float32) / np.sqrt(D_CONV).astype(np.float32)
        conv_b = 0.01 * jax.random.normal(ks[4], (D_MODEL,), jnp.float32)
        A_log = jax.random.uniform(ks[5], (D_STATE, D_MODEL), jnp.float32, minval=-3.0, maxval=-1.0)
        D_param = jnp.ones((D_MODEL,), jnp.float32)
        return {'x': x, 'W_in': W_in, 'W_out': W_out, 'conv_w': conv_w, 'conv_b': conv_b, 'A_log': A_log, 'D_param': D_param}
    _L0_attn_all = _L0_attn_setup()
    _L0_attn_in = {k: v for k, v in _L0_attn_all.items() if k in ('W_in', 'W_out', 'conv_w', 'conv_b', 'A_log', 'D_param')}
    del _L0_attn_all

    def _L0_ffn_setup():
        import jax, jax.numpy as jnp
        import numpy as np
        B, S, D, H, E = (4, 512, 256, 1024, 8)
        THRESHOLD = 0.5
        key = jax.random.key(seed)
        ks = jax.random.split(key, 7)
        s_in = 1.0 / np.sqrt(D)
        s_h = 1.0 / np.sqrt(H)
        return {'x': jax.random.normal(ks[0], (B, S, D), dtype=jnp.float32), 'Wg': jax.random.uniform(ks[1], (D, E), jnp.float32, -s_in, s_in), 'bg': jax.random.uniform(ks[2], (E,), jnp.float32, -s_in, s_in), 'W1': jax.random.uniform(ks[3], (E, D, H), jnp.float32, -s_in, s_in), 'b1': jax.random.uniform(ks[4], (E, H), jnp.float32, -s_in, s_in), 'W2': jax.random.uniform(ks[5], (E, H, D), jnp.float32, -s_h, s_h), 'b2': jax.random.uniform(ks[6], (E, D), jnp.float32, -s_h, s_h)}
    _L0_ffn_all = _L0_ffn_setup()
    _L0_ffn_in = {k: v for k, v in _L0_ffn_all.items() if k in ('Wg', 'bg', 'W1', 'b1', 'W2', 'b2')}
    del _L0_ffn_all
    return {'x': x, 'L0_tok_ln_gamma': _L0_tok_in['ln_gamma'], 'L0_tok_ln_beta': _L0_tok_in['ln_beta'], 'L0_tok_W': _L0_tok_in['W'], 'L0_tok_b': _L0_tok_in['b'], 'L0_attn_W_in': _L0_attn_in['W_in'], 'L0_attn_W_out': _L0_attn_in['W_out'], 'L0_attn_conv_w': _L0_attn_in['conv_w'], 'L0_attn_conv_b': _L0_attn_in['conv_b'], 'L0_attn_A_log': _L0_attn_in['A_log'], 'L0_attn_D_param': _L0_attn_in['D_param'], 'L0_ffn_Wg': _L0_ffn_in['Wg'], 'L0_ffn_bg': _L0_ffn_in['bg'], 'L0_ffn_W1': _L0_ffn_in['W1'], 'L0_ffn_b1': _L0_ffn_in['b1'], 'L0_ffn_W2': _L0_ffn_in['W2'], 'L0_ffn_b2': _L0_ffn_in['b2']}

def reference(x, L0_tok_ln_gamma, L0_tok_ln_beta, L0_tok_W, L0_tok_b, L0_attn_W_in, L0_attn_W_out, L0_attn_conv_w, L0_attn_conv_b, L0_attn_A_log, L0_attn_D_param, L0_ffn_Wg, L0_ffn_bg, L0_ffn_W1, L0_ffn_b1, L0_ffn_W2, L0_ffn_b2):
    import jax
    import jax.numpy as jnp

    def _L0_tok_ref(x, ln_gamma, ln_beta, W, b):
        import jax, jax.numpy as jnp
        import numpy as np
        N_EMBD = 256
        RF = 2
        FAN_IN = N_EMBD * RF
        EPS = 1e-05
        B, T, C = x.shape
        h = x.reshape(B, T // RF, C * RF)
        mu = jnp.mean(h, axis=-1, keepdims=True)
        var = jnp.mean(jnp.square(h - mu), axis=-1, keepdims=True)
        h = (h - mu) * jax.lax.rsqrt(var + EPS) * ln_gamma + ln_beta
        h = jnp.einsum('btf,ef->bte', h, W) + b
        return jax.nn.relu(h)

    def _L0_attn_ref(x, W_in, W_out, conv_w, conv_b, A_log, D_param):
        import jax, jax.numpy as jnp
        import numpy as np
        D_MODEL = 256
        D_STATE = 32
        D_CONV = 4
        BATCH = 2
        SEQ = 512

        def _forward(x, W_in, W_out, conv_w, conv_b, A_log, D_param):
            B, L, D = x.shape
            N = A_log.shape[0]
            K = conv_w.shape[-1]
            proj = x @ W_in.T
            u, delta, BC = jnp.split(proj, 3, axis=-1)
            u_c = jnp.transpose(u, (0, 2, 1))
            u_c = jax.lax.conv_general_dilated(u_c, conv_w, window_strides=(1,), padding=[(K - 1, 0)], feature_group_count=D, dimension_numbers=('NCH', 'OIH', 'NCH'))
            u = jnp.transpose(u_c, (0, 2, 1)) + conv_b[None, None, :]
            delta = jax.nn.softplus(delta)
            A_T = -jnp.exp(A_log).T
            Bm = BC[..., :N]
            Cm = BC[..., N:2 * N]

            def step(h, xt):
                d_t, b_t, c_t, u_t = xt
                h = h * jnp.exp(d_t[:, :, None] * A_T[None]) + b_t[:, None, :] * u_t[:, :, None]
                y = jnp.einsum('bdn,bn->bd', h, c_t)
                return (h, y)
            h0 = jnp.zeros((B, D, N), x.dtype)
            xs = (jnp.swapaxes(delta, 0, 1), jnp.swapaxes(Bm, 0, 1), jnp.swapaxes(Cm, 0, 1), jnp.swapaxes(u, 0, 1))
            _, ys = jax.lax.scan(step, h0, xs)
            y = jnp.swapaxes(ys, 0, 1)
            out = (y + u * D_param[None, None, :]) @ W_out.T
            return out
        return _forward(x, W_in, W_out, conv_w, conv_b, A_log, D_param)

    def _L0_ffn_ref(x, Wg, bg, W1, b1, W2, b2):
        import jax, jax.numpy as jnp
        import numpy as np
        B, S, D, H, E = (4, 512, 256, 1024, 8)
        THRESHOLD = 0.5
        b, s, d = x.shape
        x_flat = x.reshape(-1, d)
        probs = jax.nn.sigmoid(x_flat @ Wg + bg)
        mask = (probs > THRESHOLD).astype(x_flat.dtype)
        weights = probs * mask
        h = jax.nn.relu(jnp.einsum('td,edh->eth', x_flat, W1) + b1[:, None, :])
        expert_out = jnp.einsum('eth,ehd->etd', h, W2) + b2[:, None, :]
        combined = jnp.einsum('te,etd->td', weights, expert_out)
        return combined.reshape(b, s, d)
    h = _L0_tok_ref(x, L0_tok_ln_gamma, L0_tok_ln_beta, L0_tok_W, L0_tok_b)
    h = h + _L0_attn_ref(_layernorm(h, axis=-1), L0_attn_W_in, L0_attn_W_out, L0_attn_conv_w, L0_attn_conv_b, L0_attn_A_log, L0_attn_D_param)
    h = h + _L0_ffn_ref(_layernorm(h, axis=-1), L0_ffn_Wg, L0_ffn_bg, L0_ffn_W1, L0_ffn_b1, L0_ffn_W2, L0_ffn_b2)
    return h

_drawn_inputs = setup_inputs


def setup_inputs(seed=0):
    import zlib

    import numpy as np

    out = dict(_drawn_inputs(seed))
    spreads = {'L0_tok_ln_gamma': (1.0, 0.2), 'L0_tok_ln_beta': (0.0, 0.1), 'L0_attn_D_param': (1.0, 0.6)}
    factors = {'L0_attn_conv_b': 5.513,
     'L0_ffn_Wg': 3.643,
     'L0_ffn_bg': 27.481,
     'L0_ffn_W1': 3.202,
     'L0_ffn_b1': 33.19,
     'L0_ffn_b2': 26.338}
    for name, (base, spread) in spreads.items():
        noise = np.random.default_rng([zlib.crc32(name.encode()), seed]).standard_normal(out[name].shape)
        drawn = base * np.exp(spread * noise) if base else spread * noise
        out[name] = jnp.asarray(drawn.astype(out[name].dtype))
    for name, factor in factors.items():
        out[name] = (out[name] * factor).astype(out[name].dtype)
    return out
```

```python
import numpy as np
import concourse.bass as bass
from concourse import mybir
from contextlib import ExitStack

F32 = mybir.dt.float32
F16 = mybir.dt.float16
BF16 = mybir.dt.bfloat16
ALU = mybir.AluOpType
ACT = mybir.ActivationFunctionType
AX = mybir.AxisListType
RADD = bass.bass_isa.ReduceOp.add

NB = 8
D = 256
RF = 2
T = 375
NT, P = 3, 125
DH = D // 128
FK = D * RF // 128
NS = 32
CN = 2
NC = NS // CN
E = 8
H = 1024
HJ = H // 128
STEPS = E * HJ
KC = 4
EPS = 1e-5

XS = 2.0 ** 11
WCAP = 2.0 ** 14

ZR = 2
HR = 4
LAG = 2
HW = 384
SR = 3

AT_T0, AT_TOK, AT_T1, AT_U, AT_DELTA, AT_BC = 3, 5, 9, 10, 11, 12
AT_OUT, AT_T2, AT_GATE, AT_WT, AT_B2 = 58, 60, 61, 62, 63


def at_chunk(c):
    return 13 + (c * 44) // NC


CHAN = {"gamma": (FK,), "beta": (FK,), "conv_w": (DH, KC), "conv_b": (DH,), "a_log": (DH, NS), "d_par": (DH,),
        "wg": (DH, E), "b1": (E, HJ)}


def build(nc, x, tok_w, tok_b, chan, win, wout, bg, w1, w2, b2, out):
    with ExitStack() as ctx:
        def sb(name, shape, dt=F32):
            return ctx.enter_context(nc.sbuf_tensor(name, shape, dt))

        def sem(name):
            return ctx.enter_context(nc.semaphore(name))

        ident = sb("ident", [128, 128])
        pick = sb("pick", [96, NS], BF16)
        tokw_s = sb("tokw_s", [128, FK, D])
        tokb_s = sb("tokb_s", [P, D])
        win_s = sb("win_s", [128, DH, 2 * D])
        wbc_s = sb("wbc_s", [128, DH, 2, 3, NS])
        wout_s = sb("wout_s", [128, DH, D])
        chan_s = sb("chan_s", [128, chan.shape[1]])
        view, at = {}, 0
        for name, dims in CHAN.items():
            width = int(np.prod(dims))
            view[name] = chan_s[:, at:at + width]
            if len(dims) > 1:
                view[name] = view[name].rearrange("p (a b) -> p a b", a=dims[0])
            at += width
        gam_s, bet_s, cw_s, cb_s, a_s, d_s, wg_s, b1_s = view.values()
        bg_s = sb("bg_s", [P, E])
        b2_s = sb("b2_s", [E, D])
        w1p = [sb(f"w1_{p}", [128, E, DH, H], F16) for p in ("hi", "lo")]
        w2p = [sb(f"w2_{p}", [128, E, HJ, D], F16) for p in ("hi", "lo")]

        ssq = sb("ssq", [128, 3, E])
        ssr = sb("ssr", [128, 3, E])
        s_w = sb("s_w", [128, 2, E])
        i_w = sb("i_w", [128, 2, E])
        fb = sb("fb", [128, E])
        ih = sb("ih", [128, E])
        sh = sb("sh", [128, E])
        zs = sb("zs", [128, E])
        hb_s = sb("hb_s", [128, E, HJ])
        dsc = sb("dsc", [128, E])
        exps = sb("exps", [128, 3, E])
        nhalf = sb("nhalf", [P, NT])

        a_buf = sb("a_buf", [128, 2, CN, DH, T])
        x_tok = a_buf[:, :, :, :, :].rearrange("p a n h t -> p (a n h t)")[0:P, 0:NT * D * RF].rearrange(
            "p (j c) -> p j c", j=NT)
        mix = sb("mix", [128, 8 * T])
        xT0 = mix[:, 0:FK * T].rearrange("p (k t) -> p k t", k=FK)
        xh = mix[0:P, 0:NT * D].rearrange("p (j c) -> p j c", j=NT)
        xT1 = mix[:, 4 * T:6 * T].rearrange("p (k t) -> p k t", k=DH)
        bct = mix[0:96, 0:2 * T].rearrange("p (k t) -> p k t", k=2)
        bcm = mix[0:96, 2 * T:3 * T].bitcast(BF16).rearrange("p (k t) -> p k t", k=2)
        hs = mix[:, 0:CN * DH * T].rearrange("p (n h t) -> p n h t", n=CN, h=DH)
        y = mix[:, 4 * T:6 * T].rearrange("p (h t) -> p h t", h=DH)
        up0 = sb("up0", [128, DH, T + KC - 1])
        xT2 = sb("xT2", [128, DH, T])
        part = [up0[:, :, 0:T], xT2[:, :, :]]
        h0 = sb("h0", [P, NT, D])
        u = sb("u", [128, DH, T])
        dl = sb("dl", [128, DH, T])
        bcf = sb("bcf", [96, T])
        bcs = bcf[:, :].bitcast(BF16).rearrange("p (g t) -> p g t", g=2)
        st = sb("st", [P, NT, 6])
        mv = sb("mv", [P, NT, 2])
        ve = sb("ve", [P, NT])
        rs = sb("rs", [P, NT])
        gz = sb("gz", [P, NT, E])
        gw = sb("gw", [P, NT, E])
        gwt = bcf[0:E, :]
        gsc = sb("gsc", [P, NT, E])

        fa = sb("fa", [128, SR * 2048])
        raw = [fa[:, 2048 * n:2048 * (n + 1)] for n in range(SR)]
        h32 = fa[:, 0:HR * T].rearrange("p (r t) -> p r t", r=HR)
        o = HR * T
        acc = fa[0:P, o:o + NT * D].rearrange("p (j c) -> p j c", j=NT)
        o += NT * D
        tmp = fa[0:P, o:o + NT * D].rearrange("p (j c) -> p j c", j=NT)
        o += NT * D
        x2 = [fa[:, o + n * T:o + (n + 1) * T].bitcast(F16).rearrange("p (h t) -> p h t", h=DH)
              for n in range(2)]
        o += 2 * T
        hp = [fa[:, o + n * HR * HW // 2:o + (n + 1) * HR * HW // 2].bitcast(F16).rearrange(
            "p (r t) -> p r t", r=HR) for n in range(2)]
        o += HR * HW
        assert o <= SR * 2048
        gcur = sb("gcur", [P, NT, E])

        M = ctx.enter_context(nc.psum_tensor("M", [128, 4, 512], F32))
        Z = ctx.enter_context(nc.psum_tensor("Z", [128, ZR, 512], F32))
        O = ctx.enter_context(nc.psum_tensor("O", [128, 2, 512], F32))

        def rows(tile):
            return tile // 2, slice((tile % 2) * D, (tile % 2) * D + D)

        names = """const_in tokw_in ident_zero ident_set ident_ready a_exp a_ready_neg b1sq_ready pool_step
            x_in var_ready rstd_ready xhat0_ready xhat1_ready xhat2_ready xT0_psum xT0_act xT0_dve a_cleared
            tok_psum h0_ready xT1_psum xT1_ready u_psum u_padded pad_zeroed delta_psum sp_ready delta_ready bc_psum
            bchi_ready bcs_ready decay_ready B_psum C_psum bu_done scan_done ch_done part_ready y_added y_ready
            out_psum xT2_psum xT2_ready gate_psum gz_ready ge_ready gw_ready gwt_psum gwt_ready b2_psum
            base_ready gsc_ready x2hi_ready x2lo_ready gcur_ready act_step dve_step hpad_zeroed
            z_ready relu_done lo_done mm2_done evac_done acc_step acc_done acc_init out_done
            sq_done scale_done ws_ready wlo_done wscale_step hscale_ready ab_done dve_passed pool_passed""".split()
        S = {n: sem(n) for n in names}
        raw_in = [sem(f"raw_in{n}") for n in range(SR)]

        block = ctx.enter_context(nc.Block())

        x_v = x.rearrange("b (j p r) c -> b p j (r c)", j=NT, p=P, r=RF)
        out_v = out.rearrange("b (j p) c -> b p j c", j=NT, p=P)

        def wait(eng, name, value):
            if not isinstance(value, int) or value > 0:
                eng.wait_ge(S[name], value)

        consts = [(chan_s, chan),
                  (tokw_s, tok_w.rearrange("(k p) n -> p k n", p=128)),
                  (tokb_s, tok_b.partition_broadcast(P)),
                  (win_s, win[:, 0:2 * D].rearrange("(k p) n -> p k n", p=128)),
                  (wout_s, wout.rearrange("(k p) n -> p k n", p=128)),
                  (bg_s, bg.partition_broadcast(P)),
                  (b2_s, b2)]
        wbc_v = win[:, 2 * D:2 * D + 2 * NS].rearrange("(k p) (g n) -> p k g n", p=128, g=2)
        N_CONST = 16 * (len(consts) + 6)

        @block.sync
        def _(sp):
            sp.dma_start(x_tok, x_v[0]).then_inc(S["x_in"], 16)
            for n, (dst, src) in enumerate(consts):
                sp.dma_start(dst[tuple(slice(None) for _ in dst.shape)], src).then_inc(S["const_in"], 16)
            for r in range(3):
                for g in range(2):
                    sp.dma_start(wbc_s[:, :, g, r, :], wbc_v[:, :, g, :]).then_inc(S["const_in"], 16)
            for t in range(2 * E):
                wait(sp, "wlo_done", t - SR + 1)
                src = (w1[t // 2].rearrange("(k p) n -> p k n", p=128) if t % 2 == 0
                       else w2[t // 2].rearrange("(j p) n -> p j n", p=128))
                dst = raw[t % SR].rearrange("p (k n) -> p k n", k=DH if t % 2 == 0 else HJ)
                sp.dma_start(dst, src).then_inc(raw_in[t % SR], 16)

            def load_x(b):
                wait(sp, "scan_done", NC * b)
                sp.dma_start(x_tok, x_v[b]).then_inc(S["x_in"], 16)

            def store(b):
                sp.wait_ge(S["acc_done"], E * b + E + 1)
                sp.dma_start(out_v[b], acc).then_inc(S["out_done"], 16)

            load_x(1)
            with sp.Fori(1, NB - 1) as i:
                load_x(i + 1)
                store(i - 1)
            store(NB - 2)
            store(NB - 1)
            sp.wait_ge(S["out_done"], 16 * (NB + 1))

        @block.tensor
        def _(pe):
            mm = nc.tensor.matmul

            def transposes(dst, src, k, width):
                for j in range(NT):
                    last = nc.tensor.transpose(dst[0:width, j * P:(j + 1) * P],
                                               src[:, j, k * 128:k * 128 + width], ident[0:P, 0:P])
                return last

            def token_major(name, src, parts, w, bank):
                for j in range(NT):
                    b, cols = rows(j)
                    for k in range(parts):
                        last = mm(M[0:P, bank + b, cols], src[:, k, j * P:(j + 1) * P], w[:, k, :],
                                  start=(k == 0), stop=(k == parts - 1))
                    if j > 0:
                        last.then_inc(S[name], 1)

            def mixer(b, s):
                if s == AT_T0:
                    if isinstance(b, int) and b == 0:
                        pe.wait_ge(S["ident_ready"], 1)
                        pe.wait_ge(S["const_in"], N_CONST)
                    pe.wait_ge(S["xhat0_ready"], b + 1)
                    for k in range(FK):
                        transposes(M[:, k, :], x_tok, k, 128).then_inc(S["xT0_psum"], 1)
                if s == AT_TOK:
                    pe.wait_ge(S["xT0_act"], 2 * b + 2)
                    pe.wait_ge(S["xT0_dve"], 2 * b + 2)
                    token_major("tok_psum", xT0, FK, tokw_s, 0)
                if s == AT_T1:
                    pe.wait_ge(S["xhat1_ready"], b + 1)
                    for h in range(DH):
                        last = transposes(M[:, 2 + h, :], xh, h, 128)
                    last.then_inc(S["xT1_psum"], 1)
                if s == AT_U:
                    pe.wait_ge(S["xT1_ready"], b + 1)
                    project("u_psum", 0, 0)
                if s == AT_DELTA:
                    project("delta_psum", D, 2)
                if s == AT_BC:
                    pe.wait_ge(S["u_padded"], b + 1)
                    for g in range(2):
                        for k in range(DH):
                            last = mm(M[0:96, g, 0:T], wbc_s[:, k, g, :, :].rearrange("p r n -> p (r n)"), xT1[:, k, :], start=(k == 0), stop=(k == DH - 1))
                    last.then_inc(S["bc_psum"], 1)
                for c in range(NC):
                    if s == at_chunk(c):
                        if c == 0:
                            pe.wait_ge(S["bcs_ready"], b + 1)
                        else:
                            pe.wait_ge(S["bu_done"], NC * b + c)
                        spread("B_psum", 0, c)
                    if s == at_chunk(c) + 1:
                        if c == 0:
                            pe.wait_ge(S["delta_ready"], b + 1)
                        else:
                            pe.wait_ge(S["ch_done"], NC * b + c)
                        spread("C_psum", 1, c)
                if s == AT_OUT:
                    pe.wait_ge(S["y_ready"], b + 1)
                    token_major("out_psum", y, DH, wout_s, 0)
                if s == AT_T2:
                    pe.wait_ge(S["xhat2_ready"], b + 1)
                    for h in range(DH):
                        last = transposes(M[:, 2 + h, :], xh, h, 128)
                    last.then_inc(S["xT2_psum"], 1)
                if s == AT_GATE:
                    pe.wait_ge(S["xT2_ready"], b + 1)
                    for j in range(NT):
                        for k in range(DH):
                            last = mm(M[0:P, 0, j * E:(j + 1) * E], xT2[:, k, j * P:(j + 1) * P], wg_s[:, k, :],
                                      start=(k == 0), stop=(k == DH - 1))
                    last.then_inc(S["gate_psum"], 1)
                if s == AT_WT:
                    pe.wait_ge(S["gw_ready"], b + 1)
                    transposes(M[:, 1, :], gw, 0, E).then_inc(S["gwt_psum"], 1)
                if s == AT_B2:
                    pe.wait_ge(S["gwt_ready"], b + 1)
                    for j in range(NT):
                        bk, cols = rows(j)
                        last = mm(M[0:P, 2 + bk, cols], gwt[:, j * P:(j + 1) * P], b2_s[:, :], start=True, stop=True)
                    last.then_inc(S["b2_psum"], 1)

            def project(name, col, bank):
                for h in range(DH):
                    for k in range(DH):
                        last = mm(M[:, bank + h, 0:T], win_s[:, k, col + h * 128:col + (h + 1) * 128],
                                  xT1[:, k, :], start=(k == 0), stop=(k == DH - 1))
                last.then_inc(S[name], 1)

            def spread(name, g, c):
                for n in range(CN):
                    q = c * CN + n
                    last = mm(M[:, 2 * g + n, 0:T], pick[:, q:q + 1].broadcast_to([96, 128]), bcs[:, g, :],
                              start=True, stop=True)
                last.then_inc(S[name], 1)

            def first(f, s):
                e, j = s // HJ, s % HJ
                pe.wait_ge(S["relu_done"], STEPS * f + s + 1)
                n = 0
                for k in range(DH):
                    for wp, xp in ((0, 0), (0, 1), (1, 0)):
                        n += 1
                        last = mm(Z[:, s % ZR, 0:T], w1p[wp][:, e, k, j * 128:(j + 1) * 128], x2[xp][:, k, :],
                                  start=(n == 1), stop=(n == 3 * DH))
                last.then_inc(S["z_ready"], 1)

            def second(f, s):
                e, j = s // HJ, s % HJ
                if j == 0:
                    pe.wait_ge(S["evac_done"], E * f + e + 1)
                pe.wait_ge(S["lo_done"], STEPS * f + s + 1 + HR)
                for t in range(NT):
                    b, cols = rows(t)
                    for n, (hq, wp) in enumerate(((0, 0), (0, 1), (1, 0))):
                        last = mm(O[:, b, cols], hp[hq][:, s % HR, t * P:t * P + 128], w2p[wp][:, e, j, :],
                                  start=(j == 0 and n == 0 and t != 1), stop=(j == HJ - 1 and n == 2),
                                  skip_group_check=True)
                last.then_inc(S["mm2_done"], 1)

            def experts(f, s):
                first(f, s)
                if s < LAG:
                    return
                if s % HJ == LAG and s > HJ:
                    return
                if s % HJ == LAG + 1 and s > HJ:
                    second(f, s - LAG - 1)
                second(f, s - LAG)

            def tail(f):
                for s in range(STEPS - LAG, STEPS):
                    second(f, s)

            pe.sem_inc(S["mm2_done"], HR)
            for s in range(STEPS):
                mixer(0, s)
            with pe.Fori(1, NB) as i:
                pe.wait_ge(S["x2lo_ready"], i)
                for s in range(STEPS):
                    mixer(i, s)
                    experts(i - 1, s)
                tail(i - 1)
            pe.wait_ge(S["x2lo_ready"], NB)
            for s in range(STEPS):
                experts(NB - 1, s)
            tail(NB - 1)

        @block.scalar
        def _(act):
            fn = nc.scalar.activation
            ACT_STEPS = 2

            def mixer(b, s):
                if s == AT_T0 + 1:
                    for k in range(FK // 2):
                        act.wait_ge(S["xT0_psum"], FK * b + k + 1)
                        fn(xT0[:, k, :], M[:, k, 0:T], ACT.Identity, bias=bet_s[:, k:k + 1],
                           scale=gam_s[:, k:k + 1]).then_inc(S["xT0_act"], 1)
                if s == AT_T1 + 1:
                    act.wait_ge(S["xT1_psum"], b + 1)
                    fn(xT1, M[:, 2:4, 0:T], ACT.Copy).then_inc(S["xT1_ready"], 1)
                if s == AT_U + 1:
                    act.wait_ge(S["u_psum"], b + 1)
                    fn(up0[:, :, KC - 1:], M[:, 0:2, 0:T], ACT.Copy).then_inc(S["u_padded"], 1)
                if s == AT_DELTA + 1:
                    act.wait_ge(S["delta_psum"], b + 1)
                    fn(dl[:, :, :], M[:, 2:4, 0:T], ACT.Abs).then_inc(S["act_step"], 1)
                    act.wait_ge(S["act_step"], ACT_STEPS * b + 1)
                    fn(dl[:, :, :], dl[:, :, :], ACT.Exp, scale=-1.0).then_inc(S["act_step"], 1)
                    act.wait_ge(S["act_step"], ACT_STEPS * b + 2)
                    fn(dl[:, :, :], dl[:, :, :], ACT.Ln, bias=1.0).then_inc(S["sp_ready"], 1)
                if s == AT_BC + 1:
                    act.wait_ge(S["bc_psum"], b + 1)
                    fn(bcs[:, :, :], M[0:96, 0:2, 0:T], ACT.Copy).then_inc(S["bchi_ready"], 1)
                for c in range(NC):
                    if s == max(at_chunk(c) - 1, AT_BC + 1):
                        if c == 0:
                            if isinstance(b, int) and b == 0:
                                act.wait_ge(S["a_ready_neg"], 1)
                            act.wait_ge(S["delta_ready"], b + 1)
                            act.wait_ge(S["a_cleared"], b + 1)
                        if c >= 2:
                            act.wait_ge(S["scan_done"], NC * b + c - 1)
                        for n in range(CN):
                            for h in range(DH):
                                q = c * CN + n
                                last = fn(a_buf[:, c % 2, n, h, 1:T], dl[:, h, 1:T], ACT.Exp,
                                          scale=a_s[:, h, q:q + 1])
                        last.then_inc(S["decay_ready"], 1)
                if s == AT_T2 + 1:
                    act.wait_ge(S["xT2_psum"], b + 1)
                    fn(xT2[:, :, :], M[:, 2:4, 0:T], ACT.Copy, scale=XS).then_inc(S["xT2_ready"], 1)
                if s == AT_GATE + 1:
                    act.wait_ge(S["gz_ready"], b + 1)
                    fn(gz[:, :, :], gz[:, :, :], ACT.Exp, scale=-1.0).then_inc(S["ge_ready"], 1)

            def next_rows(b):
                wait(act, "z_ready", STEPS * b)
                act.wait_ge(S["xT2_ready"], b + 1)
                fn(x2[0], xT2[:, :, :], ACT.Copy).then_inc(S["x2hi_ready"], 1)

            def next_gates(b):
                act.wait_ge(S["evac_done"], E * b + 1)
                act.wait_ge(S["gsc_ready"], b + 1)
                fn(gcur[:, :, :], gsc[:, :, :], ACT.Copy).then_inc(S["gcur_ready"], 1)

            def relu(f, s):
                e, j = s // HJ, s % HJ
                act.wait_ge(S["z_ready"], STEPS * f + s + 1)
                act.wait_ge(S["lo_done"], STEPS * f + s + 1)
                args = dict(bias=hb_s[:, e, j:j + 1], scale=zs[:, e:e + 1])
                fn(h32[:, s % HR, :], Z[:, s % ZR, 0:T], ACT.Relu, **args)
                act.wait_ge(S["mm2_done"], STEPS * f + s + 1)
                fn(hp[0][:, s % HR, 0:T], Z[:, s % ZR, 0:T], ACT.Relu, **args).then_inc(S["relu_done"], 1)

            def evacuate(f, e):
                act.wait_ge(S["mm2_done"], STEPS * f + HJ * (e + 1) + HR)
                act.wait_ge(S["acc_done"], E * f + e + 1)
                act.wait_ge(S["gcur_ready"], f + 1)
                for t in range(NT):
                    b, cols = rows(t)
                    last = fn(tmp[:, t, :], O[0:P, b, cols], ACT.Copy, scale=gcur[:, t, e:e + 1])
                last.then_inc(S["evac_done"], 1)

            def experts(f, s):
                relu(f, s)
                if s % HJ == LAG - 1 and s > HJ:
                    evacuate(f, s // HJ - 1)

            def split_weights(t):
                e, kind = t // 2, t % 2
                r = raw[t % SR]
                hi = (w1p if kind == 0 else w2p)[0][:, e, :, :].rearrange("p a b -> p (a b)")
                act.wait_ge(raw_in[t % SR], 16 * (t // SR + 1))
                fn(hi, r, ACT.Square, accum_out=ssq[:, kind, e:e + 1]).then_inc(S["sq_done"], 1)
                if t > 0:
                    scale_weights(t - 1)

            def scale_weights(t):
                e, kind = t // 2, t % 2
                r = raw[t % SR]
                hi = (w1p if kind == 0 else w2p)[0][:, e, :, :].rearrange("p a b -> p (a b)")
                act.wait_ge(S["scale_done"], t + 1)
                fn(hi, r, ACT.Copy, scale=s_w[:, kind, e:e + 1])
                fn(r, r, ACT.Copy, scale=s_w[:, kind, e:e + 1]).then_inc(S["ws_ready"], 1)

            act.sem_inc(S["relu_done"], ZR)
            act.sem_inc(S["evac_done"], 1)
            act.wait_ge(S["const_in"], N_CONST)
            fn(a_s[:, :, :], a_s[:, :, :], ACT.Exp).then_inc(S["a_exp"], 1)
            act.wait_ge(S["a_exp"], 1)
            fn(a_s[:, :, :], a_s[:, :, :], ACT.Copy, scale=-1.0).then_inc(S["a_ready_neg"], 1)
            for s in range(STEPS):
                mixer(0, s)
                if s % 4 == 2:
                    split_weights(s // 4)
            scale_weights(2 * E - 1)
            act.wait_ge(S["wlo_done"], 2 * E)
            next_rows(0)
            next_gates(0)
            act.wait_ge(S["hscale_ready"], 1)
            act.wait_ge(S["hpad_zeroed"], 1)
            with act.Fori(1, NB) as i:
                for s in range(STEPS):
                    mixer(i, s)
                    if s == STEPS - 1:
                        next_rows(i)
                    experts(i - 1, s)
                evacuate(i - 1, E - 1)
                next_gates(i)
            for s in range(STEPS):
                experts(NB - 1, s)
            evacuate(NB - 1, E - 1)

        @block.vector
        def _(dve):
            v = nc.vector
            per_batch = {}

            def batch(b):
                count = [0]
                base = 0 if isinstance(b, int) and b == 0 else b * per_batch["steps"]

                def step(ins):
                    ins.then_inc(S["dve_step"], 1)
                    count[0] += 1
                    return count[0]

                def done(n):
                    dve.wait_ge(S["dve_step"], base + n)

                def norm(src, dst, nth, name):
                    for j in range(NT):
                        n = step(v.bn_stats(st[:, j, :], src[:, j, :]))
                    done(n)
                    dve.sem_inc(S["dve_passed"], 1)
                    for j in range(NT):
                        n = step(v.bn_aggr(mv[:, j, :], st[:, j, :]))
                    done(n)
                    v.tensor_scalar(ve[:, :], mv[:, :, 1], EPS, None, ALU.add).then_inc(S["var_ready"], 1)
                    dve.wait_ge(S["rstd_ready"], 3 * b + nth)
                    for j in range(NT):
                        last = v.tensor_scalar(dst[:, j, :], src[:, j, :], mv[:, j, 0:1], rs[:, j:j + 1],
                                               ALU.subtract, ALU.mult)
                    last.then_inc(S[name], 1)

                dve.wait_ge(S["x_in"], 16 * b + 16)
                norm(x_tok, x_tok, 1, "xhat0_ready")
                for k in range(FK // 2, FK):
                    dve.wait_ge(S["xT0_psum"], FK * b + k + 1)
                    v.tensor_scalar(xT0[:, k, :], M[:, k, 0:T], gam_s[:, k:k + 1], bet_s[:, k:k + 1],
                                    ALU.mult, ALU.add).then_inc(S["xT0_dve"], 1)
                a_flat = a_buf[:, :, :, :, :].rearrange("p a n h t -> p (a n h) t")
                v.memset(a_flat[:, :, 0:1], 0.0).then_inc(S["a_cleared"], 1)
                v.memset(up0[:, :, 0:KC - 1], 0.0).then_inc(S["pad_zeroed"], 1)
                wait(dve, "acc_init", b)
                for j0, w in ((0, 2), (2, 1)):
                    dve.wait_ge(S["tok_psum"], 2 * b + 1 + j0 // 2)
                    src = M[0:P, j0 // 2, 0:w * D].rearrange("p (j c) -> p j c", j=w)
                    n = step(v.tensor_tensor(h0[:, j0:j0 + w, :], src,
                                             tokb_s[:, :].unsqueeze(1).broadcast_to([P, w, D]), ALU.add))
                done(n)
                n = step(v.tensor_scalar(h0[:, :, :], h0[:, :, :], 0.0, None, ALU.max))
                done(n)
                norm(h0, xh, 2, "xhat1_ready")
                dve.wait_ge(S["u_padded"], b + 1)
                dve.wait_ge(S["pad_zeroed"], b + 1)
                for k in range(KC):
                    if k:
                        done(n)
                    for h in range(DH):
                        if k == 0:
                            n = step(v.tensor_scalar(u[:, h, :], up0[:, h, 0:T], cw_s[:, h, 0:1], cb_s[:, h:h + 1],
                                                     ALU.mult, ALU.add))
                        else:
                            n = step(v.scalar_tensor_tensor(out=u[:, h, :], in0=up0[:, h, k:k + T],
                                                            scalar=cw_s[:, h, k:k + 1], in1=u[:, h, :],
                                                            op0=ALU.mult, op1=ALU.add))
                u_done = n
                dve.wait_ge(S["sp_ready"], b + 1)
                v.scalar_tensor_tensor(out=dl[:, :, :], in0=M[:, 2:4, 0:T], scalar=0.0, in1=dl[:, :, :],
                                       op0=ALU.max, op1=ALU.add).then_inc(S["delta_ready"], 1)
                dve.wait_ge(S["bchi_ready"], b + 1)
                n = step(v.tensor_tensor(bct, M[0:96, 0:2, 0:T], bcs[:, :, :], ALU.subtract))
                done(n)
                n = step(v.tensor_copy(bcm, bct))
                done(n)
                n = step(v.tensor_copy(bcs[32:64, :, :], bcm[32:64]))
                n = step(v.tensor_tensor(bct, bct, bcm, ALU.subtract))
                done(n)
                v.tensor_copy(bcs[64:96, :, :], bct[64:96]).then_inc(S["bcs_ready"], 1)
                dve.wait_ge(S["bcs_ready"], b + 1)
                done(u_done)

                for c in range(NC):
                    dve.wait_ge(S["B_psum"], NC * b + c + 1)
                    if c > 0:
                        dve.wait_ge(S["part_ready"], NC * b + c)
                    for n in range(CN):
                        last = v.tensor_tensor(hs[:, n, :, :], u[:, :, :],
                                               M[:, n, 0:T].unsqueeze(1).broadcast_to([128, DH, T]), ALU.mult)
                    last.then_inc(S["bu_done"], 1)
                    dve.wait_ge(S["bu_done"], NC * b + c + 1)
                    dve.wait_ge(S["decay_ready"], NC * b + c + 1)
                    flat = hs.rearrange("p n h t -> p (n h t)")
                    v.tensor_tensor_scan(flat, a_buf[:, c % 2, :, :, :].rearrange("p n h t -> p (n h t)"), flat,
                                         0.0, ALU.mult, ALU.add).then_inc(S["scan_done"], 1)
                    dve.wait_ge(S["C_psum"], NC * b + c + 1)
                    dve.wait_ge(S["scan_done"], NC * b + c + 1)
                    for n in range(CN):
                        last = v.tensor_tensor(hs[:, n, :, :], hs[:, n, :, :],
                                               M[:, 2 + n, 0:T].unsqueeze(1).broadcast_to([128, DH, T]), ALU.mult)
                    last.then_inc(S["ch_done"], 1)
                    dve.wait_ge(S["ch_done"], NC * b + c + 1)
                    if c > 2:
                        dve.wait_ge(S["y_added"], (NC - 1) * b + c - 2)
                    v.tensor_tensor(y if c == 0 else part[c % 2], hs[:, 0, :, :], hs[:, 1, :, :],
                                    ALU.add).then_inc(S["part_ready"], 1)
                dve.wait_ge(S["y_added"], (NC - 1) * (b + 1))
                for h in range(DH):
                    last = v.scalar_tensor_tensor(out=y[:, h, :], in0=u[:, h, :], scalar=d_s[:, h:h + 1],
                                                  in1=y[:, h, :], op0=ALU.mult, op1=ALU.add)
                last.then_inc(S["y_ready"], 1)
                for j0, w in ((0, 2), (2, 1)):
                    dve.wait_ge(S["out_psum"], 2 * b + 1 + j0 // 2)
                    src = M[0:P, j0 // 2, 0:w * D].rearrange("p (j c) -> p j c", j=w)
                    n = step(v.tensor_tensor(h0[:, j0:j0 + w, :], src, h0[:, j0:j0 + w, :], ALU.add))
                done(n)
                norm(h0, xh, 3, "xhat2_ready")
                dve.wait_ge(S["gate_psum"], b + 1)
                gp = M[0:P, 0, 0:NT * E].rearrange("p (j e) -> p j e", j=NT)
                v.scalar_tensor_tensor(out=gz[:, :, :], in0=gp, scalar=1.0 / XS,
                                       in1=bg_s[:, :].unsqueeze(1).broadcast_to([P, NT, E]),
                                       op0=ALU.mult, op1=ALU.add).then_inc(S["gz_ready"], 1)
                dve.wait_ge(S["ge_ready"], b + 1)
                done(step(v.tensor_scalar(gz[:, :, :], gz[:, :, :], 1.0, None, ALU.add)))
                done(step(v.reciprocal(gz[:, :, :], gz[:, :, :])))
                v.scalar_tensor_tensor(out=gw[:, :, :], in0=gz[:, :, :], scalar=0.5, in1=gz[:, :, :],
                                       op0=ALU.is_gt, op1=ALU.mult).then_inc(S["gw_ready"], 1)
                dve.wait_ge(S["gw_ready"], b + 1)
                if isinstance(b, int) and b == 0:
                    dve.wait_ge(S["hscale_ready"], 1)
                wait(dve, "gcur_ready", b)
                v.tensor_tensor(gsc[:, :, :], gw[:, :, :], dsc[0:P, :].unsqueeze(1).broadcast_to([P, NT, E]),
                                ALU.mult).then_inc(S["gsc_ready"], 1)
                dve.wait_ge(S["gwt_psum"], b + 1)
                v.tensor_copy(gwt, M[0:E, 1, 0:T]).then_inc(S["gwt_ready"], 1)
                dve.wait_ge(S["b2_psum"], b + 1)
                for j0, w in ((0, 2), (2, 1)):
                    src = M[0:P, 2 + j0 // 2, 0:w * D].rearrange("p (j c) -> p j c", j=w)
                    last = v.tensor_tensor(h0[:, j0:j0 + w, :], src, h0[:, j0:j0 + w, :], ALU.add)
                last.then_inc(S["base_ready"], 1)
                dve.wait_ge(S["x2hi_ready"], b + 1)
                v.tensor_tensor(x2[1], xT2[:, :, :], x2[0], ALU.subtract).then_inc(S["x2lo_ready"], 1)
                per_batch["steps"] = count[0]

            dve.wait_ge(S["ident_ready"], 1)
            for r in range(3):
                last = v.tensor_copy(pick[32 * r:32 * (r + 1), :], ident[32 * r:32 * (r + 1), 32 * r:32 * (r + 1)])
            dve.wait_ge(S["b1sq_ready"], 1)
            v.tensor_reduce(ssq[:, 2, :], hb_s[:, :, :], AX.X, ALU.add).then_inc(S["ab_done"], 1)
            batch(0)
            with dve.Fori(1, NB) as i:
                batch(i)

        @block.gpsimd
        def _(pool):
            g = nc.gpsimd
            nstep = [0]

            def step(ins):
                nstep[0] += 1
                ins.then_inc(S["pool_step"], 1)
                pool.wait_ge(S["pool_step"], nstep[0])

            def power(b, nth):
                pool.wait_ge(S["var_ready"], 3 * b + nth)
                g.tensor_tensor(rs[:, :], ve[:, :], nhalf[:, :], ALU.pow).then_inc(S["rstd_ready"], 1)

            def mixer(b, s):
                if s == 1:
                    power(b, 1)
                if s == AT_T1 - 1:
                    power(b, 2)
                for c in range(1, NC):
                    if s == at_chunk(c) + 3:
                        pool.wait_ge(S["part_ready"], NC * b + c + 1)
                        if c > 1:
                            pool.wait_ge(S["y_added"], (NC - 1) * b + c - 1)
                        g.tensor_tensor(y, y, part[c % 2], ALU.add).then_inc(S["y_added"], 1)
                if s == AT_T2 - 1:
                    power(b, 3)

            def low(f, s):
                pool.wait_ge(S["relu_done"], STEPS * f + s + 1 + ZR)
                g.tensor_tensor(hp[1][:, s % HR, 0:T], h32[:, s % HR, :], hp[0][:, s % HR, 0:T],
                                ALU.subtract).then_inc(S["lo_done"], 1)

            def gather(f, e):
                pool.wait_ge(S["evac_done"], E * f + e + 2)
                if e > 0:
                    pool.wait_ge(S["acc_done"], E * f + e + 1)
                else:
                    pool.wait_ge(S["acc_init"], f + 1)
                g.tensor_tensor(acc, acc, tmp, ALU.add).then_inc(S["acc_done"], 1)

            def experts(f, s):
                low(f, s)
                if s == 4:
                    pool.wait_ge(S["out_done"], 16 * f + 16)
                    pool.wait_ge(S["base_ready"], f + 1)
                    pool.sem_inc(S["pool_passed"], 1)
                    g.tensor_copy(acc, h0[:, :, :]).then_inc(S["acc_init"], 1)
                if s % HJ == LAG + 1 and s > HJ:
                    gather(f, s // HJ - 1)

            def weight_scale(t):
                e, kind = t // 2, t % 2
                one = lambda z, k: z[:, k, e:e + 1]
                pool.wait_ge(S["sq_done"], t + 1)
                step(g.partition_all_reduce(one(ssr, kind), one(ssq, kind), 128, RADD))
                step(g.tensor_scalar(one(ssr, kind), one(ssr, kind), WCAP ** -2, 1e-30, ALU.mult, ALU.add))
                step(g.tensor_tensor(one(i_w, kind), one(ssr, kind), one(exps, 1), ALU.pow))
                g.tensor_tensor(one(s_w, kind), one(ssr, kind), one(exps, 0), ALU.pow).then_inc(S["scale_done"], 1)

            def weight_low(t):
                e, kind = t // 2, t % 2
                hi, lo = [w[:, e, :, :].rearrange("p a b -> p (a b)") for w in (w1p if kind == 0 else w2p)]
                pool.wait_ge(S["ws_ready"], t + 1)
                g.tensor_tensor(lo, raw[t % SR], hi, ALU.subtract).then_inc(S["wlo_done"], 1)

            def hidden_scales():
                step(g.partition_all_reduce(ssr[:, 2, :], ssq[:, 2, :], 128, RADD))
                step(g.tensor_scalar(ssr[:, 2, :], ssr[:, 2, :], WCAP ** -2, 1e-30, ALU.mult, ALU.add))
                step(g.tensor_tensor(fb[:, :], ssr[:, 2, :], exps[:, 1, :], ALU.pow))
                step(g.tensor_scalar(ih[:, :], i_w[:, 0, :], 16.0, 1.0, ALU.mult, ALU.mult))
                step(g.tensor_tensor(ih[:, :], ih[:, :], fb[:, :], ALU.add))
                step(g.tensor_tensor(sh[:, :], ih[:, :], exps[:, 2, :], ALU.pow))
                step(g.tensor_tensor(zs[:, :], sh[:, :], i_w[:, 0, :], ALU.mult))
                step(g.tensor_scalar(zs[:, :], zs[:, :], 1.0 / XS, 1.0, ALU.mult, ALU.mult))
                step(g.tensor_tensor(hb_s[:, :, :], b1_s[:, :, :], sh[:, :].unsqueeze(2).broadcast_to([128, E, HJ]),
                                     ALU.mult))
                g.tensor_tensor(dsc[:, :], ih[:, :], i_w[:, 1, :], ALU.mult).then_inc(S["hscale_ready"], 1)

            pool.sem_inc(S["lo_done"], HR)
            pool.sem_inc(S["acc_done"], 1)
            pool.sem_inc(S["out_done"], 16)
            g.memset(ident[:, :], 0.0).then_inc(S["ident_zero"], 1)
            g.memset(nhalf[:, :], -0.5)
            for n, value in enumerate((-0.5, 0.5, -1.0)):
                g.memset(exps[:, n, :], value).then_inc(S["ident_set"], 1)
            pool.wait_ge(S["ident_zero"], 1)
            pool.wait_ge(S["ident_set"], 3)
            g.affine_select(out=ident[:, :], in_=ident[:, :], compare_op=ALU.not_equal, fill=1.0, base=0,
                            pattern=[[-1, 128]], channel_multiplier=1).then_inc(S["ident_ready"], 1)
            pool.wait_ge(S["const_in"], N_CONST)
            g.tensor_tensor(hb_s[:, :, :], b1_s[:, :, :], b1_s[:, :, :], ALU.mult).then_inc(S["b1sq_ready"], 1)
            for s in range(STEPS):
                mixer(0, s)
                if s % 4 == 2:
                    weight_scale(s // 4)
                    if s > 4:
                        weight_low(s // 4 - 1)
            weight_low(2 * E - 1)
            pool.wait_ge(S["ab_done"], 1)
            hidden_scales()
            pool.wait_ge(S["wlo_done"], 2 * E)
            for n in range(2):
                last = g.memset(hp[n][:, :, T:HW], 0.0)
            last.then_inc(S["hpad_zeroed"], 1)
            with pool.Fori(1, NB) as i:
                for s in range(STEPS):
                    mixer(i, s)
                    experts(i - 1, s)
                gather(i - 1, E - 1)
            for s in range(STEPS):
                experts(NB - 1, s)
            gather(NB - 1, E - 1)


def kernel(**inputs):
    import concourse.bacc as bacc
    from concourse.bass_utils import run_bass_kernel_spmd as run

    def arr(name):
        return np.asarray(inputs[name])

    def channels(a):
        return np.moveaxis(a.reshape(a.shape[0] // 128, 128, -1), 1, 0).reshape(128, -1)

    by_channel = [arr("L0_tok_ln_gamma"), arr("L0_tok_ln_beta"), arr("L0_attn_conv_w").reshape(D, KC),
                  arr("L0_attn_conv_b"), arr("L0_attn_A_log").T, arr("L0_attn_D_param"), arr("L0_ffn_Wg"),
                  arr("L0_ffn_b1").reshape(E * H)]
    given = {
        "x": arr("x"),
        "tok_w": arr("L0_tok_W").T,
        "tok_b": arr("L0_tok_b"),
        "chan": np.concatenate([channels(a) for a in by_channel], axis=1),
        "win": arr("L0_attn_W_in").T,
        "wout": arr("L0_attn_W_out").T,
        "bg": arr("L0_ffn_bg"),
        "w1": arr("L0_ffn_W1"),
        "w2": arr("L0_ffn_W2"),
        "b2": arr("L0_ffn_b2"),
    }
    nc = bacc.Bacc("TRN2", target_bir_lowering=False, num_devices=1)
    arrays, args = {}, []
    for name, a in given.items():
        a = np.ascontiguousarray(a)
        arrays[f"in_{name}"] = a
        args.append(nc.dram_tensor(f"in_{name}", a.shape, mybir.dt.from_np(a.dtype), kind="ExternalInput").ap())
    out = nc.dram_tensor("out_0", (NB, T, D), F32, kind="ExternalOutput").ap()
    build(nc, *args, out)
    r = run(nc, [arrays], core_ids=[0])
    return r.results[0]["out_0"]
```

```python
import numpy as np
import concourse.bass as bass
from concourse import mybir
from contextlib import ExitStack

F32 = mybir.dt.float32
F16 = mybir.dt.float16
BF16 = mybir.dt.bfloat16
ALU = mybir.AluOpType
ACT = mybir.ActivationFunctionType
AX = mybir.AxisListType
RADD = bass.bass_isa.ReduceOp.add

NB = 8
D = 256
RF = 2
T = 375
NT, P = 3, 125
DH = D // 128
FK = D * RF // 128
NS = 32
NP = NS // 2
ROWS = 2 * NS
RR = 3
DR = 3
SL = 3
E = 8
H = 1024
HJ = H // 128
STEPS = E * HJ
KC = 4
EPS = 1e-5

XS = 2.0 ** 11
WCAP = 2.0 ** 14

ZR = 2
HR = 4
LAG = 2
HW = 384
SR = 6
EARLY = 2 * E - 4

AT_BC = 1
AT_SCAN, SCAN_STEPS = 4, 46
AT_OUT, AT_T2, AT_GATE, AT_WT, AT_B2 = 52, 56, 58, 60, 62


def at_row(k):
    return AT_SCAN + (k * SCAN_STEPS) // ROWS


def at_state(n):
    return AT_SCAN + (n * SCAN_STEPS) // NS


def at_pair(p):
    return AT_SCAN + (p * SCAN_STEPS) // NP


def row(k):
    if k == 0:
        return 0, 0
    if k == ROWS - 1:
        return 1, NS - 1
    return (0, (k + 1) // 2) if k % 2 else (1, k // 2 - 1)


ROW_AT = {row(k): k for k in range(ROWS)}


CHAN = {"gamma": (FK,), "beta": (FK,), "conv_w": (DH, KC), "conv_b": (DH,), "a_log": (DH, NS), "d_par": (DH,),
        "wg": (DH, E), "b1": (E, HJ)}


def build(nc, x, tok_w, tok_b, chan, win, wout, bg, w1, w2, b2, out):
    with ExitStack() as ctx:
        def sb(name, shape, dt=F32):
            return ctx.enter_context(nc.sbuf_tensor(name, shape, dt))

        def sem(name):
            return ctx.enter_context(nc.semaphore(name))

        ident = sb("ident", [128, 128])
        pick = sb("pick", [96, NS], BF16)
        tokw_s = sb("tokw_s", [128, FK, D])
        win_s = sb("win_s", [128, DH, 2 * D])
        wbc_s = sb("wbc_s", [128, DH, 2, 3, NS])
        wout_s = sb("wout_s", [128, DH, D])
        chan_s = sb("chan_s", [128, chan.shape[1]])
        view, at = {}, 0
        for name, dims in CHAN.items():
            width = int(np.prod(dims))
            view[name] = chan_s[:, at:at + width]
            if len(dims) > 1:
                view[name] = view[name].rearrange("p (a b) -> p a b", a=dims[0])
            at += width
        gam_s, bet_s, cw_s, cb_s, a_s, d_s, wg_s, b1_s = view.values()
        bg_s = sb("bg_s", [P, E])
        row_s = sb("row_s", [33, D])
        b2_s = row_s[0:E, :]
        tokb_s = row_s[32:33, :]
        one = ident[32:33, 32:33]
        w1p = [sb(f"w1_{p}", [128, E, DH, H], F16) for p in ("hi", "lo")]
        w2p = [sb(f"w2_{p}", [128, E, HJ, D], F16) for p in ("hi", "lo")]

        ssq = sb("ssq", [128, 3, E])
        ssr = sb("ssr", [128, 3, E])
        s_w = sb("s_w", [128, 2, E])
        i_w = sb("i_w", [128, 2, E])
        fb = sb("fb", [128, E])
        ih = sb("ih", [128, E])
        sh = sb("sh", [128, E])
        zs = sb("zs", [128, E])
        hb_s = sb("hb_s", [128, E, HJ])
        dsc = sb("dsc", [128, E])
        exps = sb("exps", [128, 3])
        nhalf = sb("nhalf", [P, NT])

        decay = sb("decay", [128, DR, DH, T])
        hs = sb("hs", [128, SL, DH, T])
        y = sb("y", [128, DH, T])
        up0 = sb("up0", [128, DH, T + KC - 1])
        part = up0[:, :, KC - 1:]
        u = sb("u", [128, DH, T])
        dl = sb("dl", [128, DH, T])
        h0 = sb("h0", [P, NT, D])
        bct = hs[0:96, 0, :, :]
        bcm = hs[0:96, 1, 0, :].bitcast(BF16).rearrange("p (k t) -> p k t", k=2)
        xh = hs[0:P, 0:2, :, :].rearrange("p s h t -> p (s h t)")[:, 0:NT * D].rearrange("p (j c) -> p j c", j=NT)
        xT2 = hs[:, 2, :, :]
        x_tok = sb("x_tok", [P, D * RF])
        xT0_f = sb("xT0", [128, FK * P])
        xT0 = xT0_f[:, :].rearrange("p (k t) -> p k t", k=FK)
        xh1 = xT0_f[0:P, 0:D]
        h0n = sb("h0n", [P, NT, D])
        xT1 = sb("xT1", [128, DH, T])
        stn = sb("stn", [P, 2, 6])
        mvn = sb("mvn", [P, 2, 2])
        ven = sb("ven", [P, 2])
        rsn = sb("rsn", [P, 2])
        bcf = sb("bcf", [96, T])
        bcs = bcf[:, :].bitcast(BF16).rearrange("p (g t) -> p g t", g=2)
        st = sb("st", [P, NT, 6])
        mv = sb("mv", [P, NT, 2])
        ve = sb("ve", [P, NT])
        rs = sb("rs", [P, NT])
        gz = sb("gz", [P, NT, E])
        gw = sb("gw", [P, NT, E])
        gwt = bcf[0:E, :]
        gsc = sb("gsc", [P, NT, E])

        FA = HR * T + NT * D + NT * D + 2 * T + HR * HW
        fa = sb("fa", [128, FA])
        raw = [fa[:, 2048 * n:2048 * (n + 1)] for n in range(2)]
        raw += [w[:, E - 2:E, :, :].rearrange("p e a b -> p (e a b)").bitcast(F32) for w in w1p + w2p]
        assert len(raw) == SR
        h32 = fa[:, 0:HR * T].rearrange("p (r t) -> p r t", r=HR)
        o = HR * T
        acc = fa[0:P, o:o + NT * D].rearrange("p (j c) -> p j c", j=NT)
        o += NT * D
        tmp = fa[0:P, o:o + NT * D].rearrange("p (j c) -> p j c", j=NT)
        o += NT * D
        x2 = [fa[:, o + n * T:o + (n + 1) * T].bitcast(F16).rearrange("p (h t) -> p h t", h=DH)
              for n in range(2)]
        o += 2 * T
        hp = [fa[:, o + n * HR * HW // 2:o + (n + 1) * HR * HW // 2].bitcast(F16).rearrange(
            "p (r t) -> p r t", r=HR) for n in range(2)]
        o += HR * HW
        assert o == FA and FA >= 2 * 2048
        gcur = sb("gcur", [P, NT, E])

        M = ctx.enter_context(nc.psum_tensor("M", [128, 4, 512], F32))
        Z = ctx.enter_context(nc.psum_tensor("Z", [128, ZR, 512], F32))
        X = M[:, RR, :]
        O = ctx.enter_context(nc.psum_tensor("O", [128, 2, 512], F32))

        def slot_of(t):
            if t < EARLY:
                return t % SR, t - SR
            return t % 2, t - SR if t < EARLY + 2 else t - 2

        def rows(tile):
            return tile // 2, slice((tile % 2) * D, (tile % 2) * D + D)

        names = """const_in tokw_in ident_zero ident_set ident_ready a_exp a_ready_neg b1sq_ready pool_step
            x_in var_ready rstd_ready xhat0_ready xhat1_ready xhat2_ready xT0_psum xT0_ready a_cleared
            ahead_step xvar_ready xrstd_ready hvar_ready hrstd_ready h0n_ready beta_psum tokb_ready tokw_ready

            tok_psum h0_ready xT1_psum xT1_ready u_psum u_padded pad_zeroed delta_psum sp_ready delta_ready bc_psum
            bchi_ready bcs_ready decay_ready row_ready row_used scan_done part_ready y_added y_ready
            out_psum xT2_psum xT2_ready gate_psum gz_ready ge_ready gw_ready gwt_psum gwt_ready b2_psum
            base_ready gsc_ready x2hi_ready x2lo_ready gcur_ready act_step dve_step hpad_zeroed
            z_ready relu_done lo_done mm2_done evac_done acc_step acc_done acc_init out_done
            sq_done scale_done whi_ready ws_ready wlo_done wscale_step hscale_ready ab_done dve_passed pool_passed""".split()
        S = {n: sem(n) for n in names}
        raw_in = [sem(f"raw_in{n}") for n in range(SR)]

        block = ctx.enter_context(nc.Block())

        x_v = x.rearrange("b (j p r) c -> b j p (r c)", j=NT, p=P, r=RF)
        out_v = out.rearrange("b (j p) c -> b p j c", j=NT, p=P)

        def wait(eng, name, value):
            if not isinstance(value, int) or value > 0:
                eng.wait_ge(S[name], value)

        consts = [(chan_s, chan),
                  (tokw_s, tok_w.rearrange("(k p) n -> p k n", p=128)),
                  (tokb_s, tok_b.unsqueeze(0)),
                  (win_s, win[:, 0:2 * D].rearrange("(k p) n -> p k n", p=128)),
                  (wout_s, wout.rearrange("(k p) n -> p k n", p=128)),
                  (bg_s, bg.partition_broadcast(P)),
                  (b2_s, b2)]
        wbc_v = win[:, 2 * D:2 * D + 2 * NS].rearrange("(k p) (g n) -> p k g n", p=128, g=2)
        N_CONST = 16 * (len(consts) + 6)

        @block.sync
        def _(sp):
            def load_x(b, j):
                wait(sp, "xT0_psum", NT * b + j)
                sp.dma_start(x_tok[:, :], x_v[b, j]).then_inc(S["x_in"], 16)

            def load_weights(t):
                slot, before = slot_of(t)
                wait(sp, "wlo_done", 2 * (before + 1))
                src = (w1[t // 2].rearrange("(k p) n -> p k n", p=128) if t % 2 == 0
                       else w2[t // 2].rearrange("(j p) n -> p j n", p=128))
                dst = raw[slot].rearrange("p (k n) -> p k n", k=DH if t % 2 == 0 else HJ)
                sp.dma_start(dst, src).then_inc(raw_in[slot], 16)

            def store(b):
                sp.wait_ge(S["acc_done"], NT * E * (b + 1) + NT)
                sp.dma_start(out_v[b], acc).then_inc(S["out_done"], 16)

            load_x(0, 0)
            for n, (dst, src) in enumerate(consts):
                sp.dma_start(dst[tuple(slice(None) for _ in dst.shape)], src).then_inc(S["const_in"], 16)
            for r in range(3):
                for g in range(2):
                    sp.dma_start(wbc_s[:, :, g, r, :], wbc_v[:, :, g, :]).then_inc(S["const_in"], 16)
            load_weights(0)
            load_x(0, 1)
            load_weights(1)
            load_x(0, 2)
            load_weights(2)
            load_x(1, 0)
            for t in range(3, SR):
                load_weights(t)
            for t in range(SR, 2 * E):
                load_weights(t)
                if t == 7:
                    load_x(1, 1)
                if t == 11:
                    load_x(1, 2)
            with sp.Fori(1, NB - 1) as i:
                for j in range(NT):
                    load_x(i + 1, j)
                store(i - 1)
            store(NB - 2)
            store(NB - 1)
            sp.wait_ge(S["out_done"], 16 * (NB + 1))

        @block.tensor
        def _(pe):
            mm = nc.tensor.matmul

            def transposes(dst, src, k, width):
                for j in range(NT):
                    last = nc.tensor.transpose(dst[0:width, j * P:(j + 1) * P],
                                               src[:, j, k * 128:k * 128 + width], ident[0:P, 0:P])
                return last

            def token_major(name, src, parts, w, bank):
                for j in range(NT):
                    b, cols = rows(j)
                    for k in range(parts):
                        last = mm(M[0:P, bank + b, cols], src[:, k, j * P:(j + 1) * P], w[:, k, :],
                                  start=(k == 0), stop=(k == parts - 1))
                    if j > 0:
                        last.then_inc(S[name], 1)

            def turn_x(b, j):
                pe.wait_ge(S["xhat0_ready"], NT * b + j + 1)
                wait(pe, "xT1_ready", NT * b + j)
                for k in range(FK):
                    last = nc.tensor.transpose(X[:, k * P:(k + 1) * P], x_tok[:, k * 128:(k + 1) * 128],
                                               ident[0:P, 0:P])
                last.then_inc(S["xT0_psum"], 1)

            def tokens(b, j):
                pe.wait_ge(S["xT0_ready"], NT * b + j + 1)
                mm(X[0:P, 0:D], one.broadcast_to([1, P]), tokb_s[:, :], start=True, stop=False)
                for k in range(FK):
                    last = mm(X[0:P, 0:D], xT0[:, k, :], tokw_s[:, k, :], start=False, stop=(k == FK - 1))
                last.then_inc(S["tok_psum"], 1)

            def turn_tokens(b, j):
                pe.wait_ge(S["xhat1_ready"], NT * b + j + 1)
                for h in range(DH):
                    last = nc.tensor.transpose(X[:, D + h * P:D + (h + 1) * P], xh1[:, h * 128:(h + 1) * 128],
                                               ident[0:P, 0:P])
                last.then_inc(S["xT1_psum"], 1)

            def ahead(b, s):
                for j in range(NT):
                    if s == at_pair(5 * j + 1) + 1:
                        turn_x(b + 1, j)
                    if s == at_pair(5 * j + 1) + 3:
                        tokens(b + 1, j)
                    if s == at_pair(5 * j + 4) + 1:
                        turn_tokens(b + 1, j)

            def mixer(b, s, more):
                if s == 0:
                    pe.wait_ge(S["xT1_ready"], NT * b + NT)
                    wait(pe, "base_ready", b)
                    project("u_psum", 0, 0)
                    project("delta_psum", D, 2)
                if s == AT_BC:
                    pe.wait_ge(S["u_padded"], b + 1)
                    for g in range(2):
                        for k in range(DH):
                            last = mm(M[0:96, g, 0:T], wbc_s[:, k, g, :, :].rearrange("p r n -> p (r n)"), xT1[:, k, :], start=(k == 0), stop=(k == DH - 1))
                    last.then_inc(S["bc_psum"], 1)
                for k in range(ROWS):
                    if s == at_row(k):
                        spread(b, k)
                if more:
                    ahead(b, s)
                if s == AT_OUT:
                    pe.wait_ge(S["y_ready"], b + 1)
                    token_major("out_psum", y, DH, wout_s, 0)
                if s == AT_T2:
                    pe.wait_ge(S["xhat2_ready"], b + 1)
                    if more:
                        pe.wait_ge(S["xT1_ready"], NT * b + 2 * NT)
                    for h in range(DH):
                        last = transposes(M[:, 2 + h, :], xh, h, 128)
                    last.then_inc(S["xT2_psum"], 1)
                if s == AT_GATE:
                    pe.wait_ge(S["xT2_ready"], b + 1)
                    for j in range(NT):
                        for k in range(DH):
                            last = mm(M[0:P, 0, j * E:(j + 1) * E], xT2[:, k, j * P:(j + 1) * P], wg_s[:, k, :],
                                      start=(k == 0), stop=(k == DH - 1))
                    last.then_inc(S["gate_psum"], 1)
                if s == AT_WT:
                    pe.wait_ge(S["gw_ready"], b + 1)
                    transposes(M[:, 1, :], gw, 0, E).then_inc(S["gwt_psum"], 1)
                if s == AT_B2:
                    pe.wait_ge(S["gwt_ready"], b + 1)
                    for j in range(NT):
                        bk, cols = rows(j)
                        last = mm(M[0:P, 2 + bk, cols], gwt[:, j * P:(j + 1) * P], b2_s[:, :], start=True, stop=True)
                    last.then_inc(S["b2_psum"], 1)

            def project(name, col, bank):
                for h in range(DH):
                    for k in range(DH):
                        last = mm(M[:, bank + h, 0:T], win_s[:, k, col + h * 128:col + (h + 1) * 128],
                                  xT1[:, k, :], start=(k == 0), stop=(k == DH - 1))
                last.then_inc(S[name], 1)

            def spread(b, k):
                g, n = row(k)
                if k == 0:
                    pe.wait_ge(S["bcs_ready"], b + 1)
                if k == 2:
                    pe.wait_ge(S["delta_ready"], b + 1)
                if k >= RR:
                    pe.wait_ge(S["row_used"], ROWS * b + k - RR + 1)
                mm(M[:, k % RR, 0:T], pick[:, n:n + 1].broadcast_to([96, 128]), bcs[:, g, :],
                   start=True, stop=True).then_inc(S["row_ready"], 1)

            def first(f, s):
                e, j = s // HJ, s % HJ
                pe.wait_ge(S["relu_done"], STEPS * f + s + 1)
                n = 0
                for k in range(DH):
                    for wp, xp in ((0, 0), (0, 1), (1, 0)):
                        n += 1
                        last = mm(Z[:, s % ZR, 0:T], w1p[wp][:, e, k, j * 128:(j + 1) * 128], x2[xp][:, k, :],
                                  start=(n == 1), stop=(n == 3 * DH))
                last.then_inc(S["z_ready"], 1)

            def second(f, s):
                e, j = s // HJ, s % HJ
                if j == 0:
                    pe.wait_ge(S["evac_done"], NT * (E * f + e) + 1)
                pe.wait_ge(S["lo_done"], STEPS * f + s + 1 + HR)
                for t in range(NT):
                    b, cols = rows(t)
                    for n, (hq, wp) in enumerate(((0, 0), (0, 1), (1, 0))):
                        last = mm(O[:, b, cols], hp[hq][:, s % HR, t * P:t * P + 128], w2p[wp][:, e, j, :],
                                  start=(j == 0 and n == 0 and t != 1), stop=(j == HJ - 1 and n == 2),
                                  skip_group_check=True)
                last.then_inc(S["mm2_done"], 1)

            def experts(f, s):
                first(f, s)
                if s < LAG:
                    return
                if s % HJ == LAG and s > HJ:
                    return
                if s % HJ == LAG + 1 and s > HJ:
                    second(f, s - LAG - 1)
                second(f, s - LAG)

            def tail(f):
                for s in range(STEPS - LAG, STEPS):
                    second(f, s)

            pe.sem_inc(S["mm2_done"], HR)
            pe.wait_ge(S["ident_ready"], 1)
            pe.wait_ge(S["const_in"], N_CONST)
            for k in range(FK):
                mm(M[0:1, 0, 0:D], bet_s[:, k:k + 1], tokw_s[:, k, :], start=(k == 0), stop=False)
            mm(M[0:1, 0, 0:D], one, tokb_s, start=False, stop=True).then_inc(S["beta_psum"], 1)
            turn_x(0, 0)
            pe.wait_ge(S["tokb_ready"], 1)
            pe.wait_ge(S["tokw_ready"], 1)
            for j in range(NT):
                if j > 0:
                    turn_x(0, j)
                tokens(0, j)
                turn_tokens(0, j)
            for s in range(STEPS):
                mixer(0, s, True)

            def both(b, more):
                mixer(b, 0, more)
                pe.wait_ge(S["x2lo_ready"], b)
                experts(b - 1, 0)
                for s in range(1, STEPS):
                    mixer(b, s, more)
                    experts(b - 1, s)
                tail(b - 1)

            with pe.Fori(1, NB - 1) as i:
                both(i, True)
            both(NB - 1, False)
            pe.wait_ge(S["x2lo_ready"], NB)
            for s in range(STEPS):
                experts(NB - 1, s)
            tail(NB - 1)

        @block.scalar
        def _(act):
            fn = nc.scalar.activation
            ACT_STEPS = 2
            AT_H0 = AT_SCAN + 4

            def input_turned(b, j):
                act.wait_ge(S["xT0_psum"], NT * b + j + 1)
                fn(xT0_f[:, :], X[:, 0:FK * P], ACT.Copy).then_inc(S["xT0_ready"], 1)

            def token_rows(b, j):
                act.wait_ge(S["tok_psum"], NT * b + j + 1)
                wait(act, "h0_ready", b)
                fn(h0n[:, j, :], X[0:P, 0:D], ACT.Relu).then_inc(S["h0n_ready"], 1)

            def tokens_turned(b, j):
                act.wait_ge(S["xT1_psum"], NT * b + j + 1)
                wait(act, "bc_psum", b)
                fn(xT1[:, :, j * P:(j + 1) * P], X[:, D:D + DH * P].rearrange("p (h t) -> p h t", h=DH),
                   ACT.Copy).then_inc(S["xT1_ready"], 1)

            def ahead(b, s):
                for j in range(NT):
                    if s == at_pair(5 * j + 1) + 2:
                        input_turned(b + 1, j)
                    if s == at_pair(5 * j + 1) + 4:
                        token_rows(b + 1, j)
                    if s == at_pair(5 * j + 4) + 2:
                        tokens_turned(b + 1, j)

            def mixer(b, s, more):
                if s == 0:
                    act.wait_ge(S["u_psum"], b + 1)
                    fn(up0[:, :, KC - 1:], M[:, 0:2, 0:T], ACT.Copy).then_inc(S["u_padded"], 1)
                    act.wait_ge(S["delta_psum"], b + 1)
                    fn(dl[:, :, :], M[:, 2:4, 0:T], ACT.Abs).then_inc(S["act_step"], 1)
                    act.wait_ge(S["act_step"], ACT_STEPS * b + 1)
                    fn(dl[:, :, :], dl[:, :, :], ACT.Exp, scale=-1.0).then_inc(S["act_step"], 1)
                    act.wait_ge(S["act_step"], ACT_STEPS * b + 2)
                    fn(dl[:, :, :], dl[:, :, :], ACT.Ln, bias=1.0).then_inc(S["sp_ready"], 1)
                if s == AT_BC:
                    act.wait_ge(S["bc_psum"], b + 1)
                    fn(bcs[:, :, :], M[0:96, 0:2, 0:T], ACT.Copy).then_inc(S["bchi_ready"], 1)
                for n in range(NS):
                    if s == max(at_state(n) - 1, AT_BC):
                        if n == 0:
                            if isinstance(b, int) and b == 0:
                                act.wait_ge(S["a_ready_neg"], 1)
                            act.wait_ge(S["delta_ready"], b + 1)
                            act.wait_ge(S["a_cleared"], 1)
                        if n >= DR:
                            act.wait_ge(S["scan_done"], NS * b + n - DR + 1)
                        for h in range(DH):
                            last = fn(decay[:, n % DR, h, 1:T], dl[:, h, 1:T], ACT.Exp, scale=a_s[:, h, n:n + 1])
                        last.then_inc(S["decay_ready"], 1)
                if s == AT_H0:
                    act.wait_ge(S["h0n_ready"], NT * b + NT)
                    wait(act, "acc_init", b)
                    fn(h0[:, :, :], h0n[:, :, :], ACT.Copy).then_inc(S["h0_ready"], 1)
                if more:
                    ahead(b, s)
                if s == AT_T2 + 1:
                    act.wait_ge(S["xT2_psum"], b + 1)
                    fn(xT2[:, :, :], M[:, 2:4, 0:T], ACT.Copy, scale=XS).then_inc(S["xT2_ready"], 1)
                if s == AT_GATE + 1:
                    act.wait_ge(S["gz_ready"], b + 1)
                    fn(gz[:, :, :], gz[:, :, :], ACT.Exp, scale=-1.0).then_inc(S["ge_ready"], 1)

            def next_rows(b):
                wait(act, "z_ready", STEPS * b)
                act.wait_ge(S["xT2_ready"], b + 1)
                fn(x2[0], xT2[:, :, :], ACT.Copy).then_inc(S["x2hi_ready"], 1)

            def next_gates(b):
                act.wait_ge(S["evac_done"], NT * E * b + 1)
                act.wait_ge(S["gsc_ready"], b + 1)
                fn(gcur[:, :, :], gsc[:, :, :], ACT.Copy).then_inc(S["gcur_ready"], 1)

            def relu(f, s):
                e, j = s // HJ, s % HJ
                act.wait_ge(S["z_ready"], STEPS * f + s + 1)
                act.wait_ge(S["lo_done"], STEPS * f + s + 1)
                args = dict(bias=hb_s[:, e, j:j + 1], scale=zs[:, e:e + 1])
                fn(h32[:, s % HR, :], Z[:, s % ZR, 0:T], ACT.Relu, **args)
                act.wait_ge(S["mm2_done"], STEPS * f + s + 1)
                fn(hp[0][:, s % HR, 0:T], Z[:, s % ZR, 0:T], ACT.Relu, **args).then_inc(S["relu_done"], 1)

            def evacuate(f, e):
                act.wait_ge(S["mm2_done"], STEPS * f + HJ * (e + 1) + HR)
                act.wait_ge(S["gcur_ready"], f + 1)
                for t in range(NT):
                    b, cols = rows(t)
                    act.wait_ge(S["acc_done"], NT * (E * f + e) + t + 1)
                    fn(tmp[:, t, :], O[0:P, b, cols], ACT.Copy,
                       scale=gcur[:, t, e:e + 1]).then_inc(S["evac_done"], 1)

            def experts(f, s):
                relu(f, s)
                if s % HJ == LAG - 1 and s > HJ:
                    evacuate(f, s // HJ - 1)

            def square_weights(t):
                e, kind = t // 2, t % 2
                slot, before = slot_of(t)
                hi = (w1p if kind == 0 else w2p)[0][:, e, :, :].rearrange("p a b -> p (a b)")
                act.wait_ge(raw_in[slot], 16 * (t // SR + 1 if t < EARLY + 2 else EARLY // SR + 2))
                if t >= EARLY:
                    act.wait_ge(S["wlo_done"], 2 * EARLY - 4 * (1 - kind))
                fn(hi, raw[slot], ACT.Square, accum_out=ssq[:, kind, e:e + 1]).then_inc(S["sq_done"], 1)

            def weight_high(t):
                e, kind = t // 2, t % 2
                hi = (w1p if kind == 0 else w2p)[0][:, e, :, :].rearrange("p a b -> p (a b)")
                act.wait_ge(S["scale_done"], t + 1)
                fn(hi, raw[slot_of(t)[0]], ACT.Copy, scale=s_w[:, kind, e:e + 1]).then_inc(S["whi_ready"], 1)

            def scale_weights(t):
                e, kind = t // 2, t % 2
                r = raw[slot_of(t)[0]]
                act.wait_ge(S["whi_ready"], t + 1)
                fn(r, r, ACT.Copy, scale=s_w[:, kind, e:e + 1]).then_inc(S["ws_ready"], 1)

            def prepare(s):
                t = s // 3
                if s % 3 == 0 and t < 2 * E:
                    square_weights(t)
                if s % 3 == 1 and 0 < t <= 2 * E:
                    weight_high(t - 1)
                if s % 3 == 2 and 0 < t <= 2 * E:
                    scale_weights(t - 1)

            nc.scalar.preload_act_table_set("natural_log_exp_and_others")
            act.sem_inc(S["relu_done"], ZR)
            act.sem_inc(S["evac_done"], 1)
            act.wait_ge(S["const_in"], N_CONST)
            fn(a_s[:, :, :], a_s[:, :, :], ACT.Exp).then_inc(S["a_exp"], 1)
            act.wait_ge(S["a_exp"], 1)
            fn(a_s[:, :, :], a_s[:, :, :], ACT.Copy, scale=-1.0).then_inc(S["a_ready_neg"], 1)
            for j in range(NT):
                input_turned(0, j)
                token_rows(0, j)
                tokens_turned(0, j)
            for s in range(STEPS):
                mixer(0, s, True)
                prepare(s)
            act.wait_ge(S["wlo_done"], 4 * E)
            next_rows(0)
            next_gates(0)
            act.wait_ge(S["hscale_ready"], 1)
            act.wait_ge(S["hpad_zeroed"], 1)

            def both(b, more):
                for s in range(STEPS):
                    mixer(b, s, more)
                    experts(b - 1, s)
                next_rows(b)
                evacuate(b - 1, E - 1)
                next_gates(b)

            with act.Fori(1, NB - 1) as i:
                both(i, True)
            both(NB - 1, False)
            for s in range(STEPS):
                experts(NB - 1, s)
            evacuate(NB - 1, E - 1)

        @block.vector
        def _(dve):
            v = nc.vector
            per_batch = {}

            NORM = ({"variance": "xvar_ready", "rstd": "xrstd_ready", "rows": "xhat0_ready"},
                    {"variance": "hvar_ready", "rstd": "hrstd_ready", "rows": "xhat1_ready"})

            def stats(b, j, which):
                if which == 0:
                    dve.wait_ge(S["x_in"], 16 * (NT * b + j + 1))
                else:
                    dve.wait_ge(S["h0n_ready"], NT * b + j + 1)
                v.bn_stats(stn[:, which, :], x_tok[:, :] if which == 0 else h0n[:, j, :]).then_inc(S["ahead_step"], 1)

            def moments(b, j, which):
                wait(dve, NORM[which]["rows"], NT * b + j)
                dve.wait_ge(S["ahead_step"], 4 * (NT * b + j) + 2 * which + 1)
                dve.sem_inc(S["dve_passed"], 1)
                v.bn_aggr(mvn[:, which, :], stn[:, which, :]).then_inc(S["ahead_step"], 1)

            def variance(b, j, which):
                dve.wait_ge(S["ahead_step"], 4 * (NT * b + j) + 2 * which + 2)
                v.tensor_scalar(ven[:, which:which + 1], mvn[:, which, 1:2], EPS, None,
                                ALU.add).then_inc(S[NORM[which]["variance"]], 1)

            def normalise(b, j, which):
                dve.wait_ge(S[NORM[which]["rstd"]], NT * b + j + 1)
                src, dst = (x_tok[:, :], x_tok[:, :]) if which == 0 else (h0n[:, j, :], xh1)
                v.tensor_scalar(dst, src, mvn[:, which, 0:1], rsn[:, which:which + 1],
                                ALU.subtract, ALU.mult).then_inc(S[NORM[which]["rows"]], 1)

            def batch(b, more):
                count = [0]
                base = 0 if isinstance(b, int) and b == 0 else b * per_batch["steps"]

                def step(ins):
                    ins.then_inc(S["dve_step"], 1)
                    count[0] += 1
                    return count[0]

                def done(n):
                    dve.wait_ge(S["dve_step"], base + n)

                def norm(src, dst, name):
                    for j in range(NT):
                        n = step(v.bn_stats(st[:, j, :], src[:, j, :]))
                    done(n)
                    dve.sem_inc(S["dve_passed"], 1)
                    for j in range(NT):
                        n = step(v.bn_aggr(mv[:, j, :], st[:, j, :]))
                    done(n)
                    v.tensor_scalar(ve[:, :], mv[:, :, 1], EPS, None, ALU.add).then_inc(S["var_ready"], 1)
                    dve.wait_ge(S["rstd_ready"], b + 1)
                    for j in range(NT):
                        last = v.tensor_scalar(dst[:, j, :], src[:, j, :], mv[:, j, 0:1], rs[:, j:j + 1],
                                               ALU.subtract, ALU.mult)
                    last.then_inc(S[name], 1)

                dve.wait_ge(S["u_padded"], b + 1)
                if isinstance(b, int) and b == 0:
                    dve.wait_ge(S["pad_zeroed"], 1)
                wait(dve, "x2lo_ready", b)
                for k in range(KC):
                    if k:
                        done(n)
                    for h in range(DH):
                        if k == 0:
                            n = step(v.tensor_scalar(u[:, h, :], up0[:, h, 0:T], cw_s[:, h, 0:1], cb_s[:, h:h + 1],
                                                     ALU.mult, ALU.add))
                        else:
                            n = step(v.scalar_tensor_tensor(out=u[:, h, :], in0=up0[:, h, k:k + T],
                                                            scalar=cw_s[:, h, k:k + 1], in1=u[:, h, :],
                                                            op0=ALU.mult, op1=ALU.add))
                u_done = n
                dve.wait_ge(S["sp_ready"], b + 1)
                v.scalar_tensor_tensor(out=dl[:, :, :], in0=M[:, 2:4, 0:T], scalar=0.0, in1=dl[:, :, :],
                                       op0=ALU.max, op1=ALU.add).then_inc(S["delta_ready"], 1)
                dve.wait_ge(S["bchi_ready"], b + 1)
                n = step(v.tensor_tensor(bct, M[0:96, 0:2, 0:T], bcs[:, :, :], ALU.subtract))
                done(n)
                n = step(v.tensor_copy(bcm, bct))
                done(n)
                n = step(v.tensor_copy(bcs[32:64, :, :], bcm[32:64]))
                n = step(v.tensor_tensor(bct, bct, bcm, ALU.subtract))
                done(n)
                v.tensor_copy(bcs[64:96, :, :], bct[64:96]).then_inc(S["bcs_ready"], 1)
                dve.wait_ge(S["bcs_ready"], b + 1)
                done(u_done)

                def drive(n):
                    k = ROW_AT[0, n]
                    dve.wait_ge(S["row_ready"], ROWS * b + k + 1)
                    if n >= SL:
                        dve.wait_ge(S["part_ready"], NP * b + (n - SL) // 2 + 1)
                    v.tensor_tensor(hs[:, n % SL, :, :], u[:, :, :],
                                    M[:, k % RR, 0:T].unsqueeze(1).broadcast_to([128, DH, T]),
                                    ALU.mult).then_inc(S["row_used"], 1)

                def scan(n):
                    dve.wait_ge(S["row_used"], ROWS * b + ROW_AT[0, n] + 1)
                    dve.wait_ge(S["decay_ready"], NS * b + n + 1)
                    flat = hs[:, n % SL, :, :].rearrange("p h t -> p (h t)")
                    v.tensor_tensor_scan(flat, decay[:, n % DR, :, :].rearrange("p h t -> p (h t)"), flat,
                                         0.0, ALU.mult, ALU.add).then_inc(S["scan_done"], 1)

                def weigh(n):
                    k = ROW_AT[1, n]
                    dve.wait_ge(S["row_ready"], ROWS * b + k + 1)
                    dve.wait_ge(S["scan_done"], NS * b + n + 1)
                    v.tensor_tensor(hs[:, n % SL, :, :], hs[:, n % SL, :, :],
                                    M[:, k % RR, 0:T].unsqueeze(1).broadcast_to([128, DH, T]),
                                    ALU.mult).then_inc(S["row_used"], 1)

                def pair_sum(p):
                    dve.wait_ge(S["row_used"], ROWS * b + ROW_AT[1, 2 * p + 1] + 1)
                    if p > 1:
                        dve.wait_ge(S["y_added"], (NP - 1) * b + p - 1)
                    v.tensor_tensor(y[:, :, :] if p == 0 else part, hs[:, 2 * p % SL, :, :],
                                    hs[:, (2 * p + 1) % SL, :, :], ALU.add).then_inc(S["part_ready"], 1)

                drive(0)
                scan(0)
                for p in range(NP):
                    if more and p % 5 in (1, 4) and p < 5 * NT:
                        normalise(b + 1, p // 5, p % 5 // 4)
                    drive(2 * p + 1)
                    if more and p % 5 in (0, 3) and p < 5 * NT:
                        stats(b + 1, p // 5, p % 5 // 3)
                    weigh(2 * p)
                    scan(2 * p + 1)
                    if more and p % 5 in (0, 3) and p < 5 * NT:
                        moments(b + 1, p // 5, p % 5 // 3)
                    if p < NP - 1:
                        drive(2 * p + 2)
                    weigh(2 * p + 1)
                    if more and p % 5 in (0, 3) and p < 5 * NT:
                        variance(b + 1, p // 5, p % 5 // 3)
                    if p < NP - 1:
                        scan(2 * p + 2)
                    pair_sum(p)
                dve.wait_ge(S["y_added"], (NP - 1) * (b + 1))
                for h in range(DH):
                    last = v.scalar_tensor_tensor(out=y[:, h, :], in0=u[:, h, :], scalar=d_s[:, h:h + 1],
                                                  in1=y[:, h, :], op0=ALU.mult, op1=ALU.add)
                last.then_inc(S["y_ready"], 1)
                dve.wait_ge(S["h0_ready"], b + 1)
                for j0, w in ((0, 2), (2, 1)):
                    dve.wait_ge(S["out_psum"], 2 * b + 1 + j0 // 2)
                    src = M[0:P, j0 // 2, 0:w * D].rearrange("p (j c) -> p j c", j=w)
                    n = step(v.tensor_tensor(h0[:, j0:j0 + w, :], src, h0[:, j0:j0 + w, :], ALU.add))
                done(n)
                norm(h0, xh, "xhat2_ready")
                dve.wait_ge(S["gate_psum"], b + 1)
                gp = M[0:P, 0, 0:NT * E].rearrange("p (j e) -> p j e", j=NT)
                v.scalar_tensor_tensor(out=gz[:, :, :], in0=gp, scalar=1.0 / XS,
                                       in1=bg_s[:, :].unsqueeze(1).broadcast_to([P, NT, E]),
                                       op0=ALU.mult, op1=ALU.add).then_inc(S["gz_ready"], 1)
                dve.wait_ge(S["ge_ready"], b + 1)
                done(step(v.tensor_scalar(gz[:, :, :], gz[:, :, :], 1.0, None, ALU.add)))
                done(step(v.reciprocal(gz[:, :, :], gz[:, :, :])))
                v.scalar_tensor_tensor(out=gw[:, :, :], in0=gz[:, :, :], scalar=0.5, in1=gz[:, :, :],
                                       op0=ALU.is_gt, op1=ALU.mult).then_inc(S["gw_ready"], 1)
                dve.wait_ge(S["gw_ready"], b + 1)
                if isinstance(b, int) and b == 0:
                    dve.wait_ge(S["hscale_ready"], 1)
                wait(dve, "gcur_ready", b)
                v.tensor_tensor(gsc[:, :, :], gw[:, :, :], dsc[0:P, :].unsqueeze(1).broadcast_to([P, NT, E]),
                                ALU.mult).then_inc(S["gsc_ready"], 1)
                dve.wait_ge(S["gwt_psum"], b + 1)
                v.tensor_copy(gwt, M[0:E, 1, 0:T]).then_inc(S["gwt_ready"], 1)
                dve.wait_ge(S["b2_psum"], b + 1)
                for j0, w in ((0, 2), (2, 1)):
                    src = M[0:P, 2 + j0 // 2, 0:w * D].rearrange("p (j c) -> p j c", j=w)
                    last = v.tensor_tensor(h0[:, j0:j0 + w, :], src, h0[:, j0:j0 + w, :], ALU.add)
                last.then_inc(S["base_ready"], 1)
                dve.wait_ge(S["x2hi_ready"], b + 1)
                v.tensor_tensor(x2[1], xT2[:, :, :], x2[0], ALU.subtract).then_inc(S["x2lo_ready"], 1)
                per_batch["steps"] = count[0]

            dve.wait_ge(S["ident_ready"], 1)
            for r in range(3):
                last = v.tensor_copy(pick[32 * r:32 * (r + 1), :], ident[32 * r:32 * (r + 1), 32 * r:32 * (r + 1)])
            dve.wait_ge(S["b1sq_ready"], 1)
            v.tensor_reduce(ssq[:, 2, :], hb_s[:, :, :], AX.X, ALU.add).then_inc(S["ab_done"], 1)
            v.memset(decay[:, :, :, :].rearrange("p a h t -> p (a h) t")[:, :, 0:1], 0.0).then_inc(S["a_cleared"], 1)
            v.memset(up0[:, :, 0:KC - 1], 0.0).then_inc(S["pad_zeroed"], 1)
            stats(0, 0, 0)
            moments(0, 0, 0)
            variance(0, 0, 0)
            normalise(0, 0, 0)
            dve.wait_ge(S["beta_psum"], 1)
            v.tensor_copy(tokb_s, M[0:1, 0, 0:D]).then_inc(S["tokb_ready"], 1)
            v.tensor_tensor(tokw_s[:, :, :], tokw_s[:, :, :], gam_s.unsqueeze(2).broadcast_to([128, FK, D]),
                            ALU.mult).then_inc(S["tokw_ready"], 1)
            for j in range(NT):
                for which in range(2):
                    if j + which > 0:
                        stats(0, j, which)
                        moments(0, j, which)
                        variance(0, j, which)
                        normalise(0, j, which)
            batch(0, True)
            with dve.Fori(1, NB - 1) as i:
                batch(i, True)
            batch(NB - 1, False)

        @block.gpsimd
        def _(pool):
            g = nc.gpsimd
            nstep = [0]

            def step(ins):
                nstep[0] += 1
                ins.then_inc(S["pool_step"], 1)
                pool.wait_ge(S["pool_step"], nstep[0])

            def ahead_power(b, j, which):
                pool.wait_ge(S["hvar_ready" if which else "xvar_ready"], NT * b + j + 1)
                g.tensor_tensor(rsn[:, which:which + 1], ven[:, which:which + 1], nhalf[:, 0:1],
                                ALU.pow).then_inc(S["hrstd_ready" if which else "xrstd_ready"], 1)

            def power(b):
                pool.wait_ge(S["var_ready"], b + 1)
                g.tensor_tensor(rs[:, :], ve[:, :], nhalf[:, :], ALU.pow).then_inc(S["rstd_ready"], 1)

            def mixer(b, s, more):
                for p in range(NP):
                    if more and s == at_pair(p) + 2 and p % 5 in (0, 3) and p < 5 * NT:
                        ahead_power(b + 1, p // 5, p % 5 // 3)
                    if s == at_pair(p) + 3 and p > 0:
                        pool.wait_ge(S["part_ready"], NP * b + p + 1)
                        if p > 1:
                            pool.wait_ge(S["y_added"], (NP - 1) * b + p - 1)
                        g.tensor_tensor(y[:, :, :], y[:, :, :], part, ALU.add).then_inc(S["y_added"], 1)
                if s == AT_T2 - 2:
                    power(b)

            def low(f, s):
                pool.wait_ge(S["relu_done"], STEPS * f + s + 1 + ZR)
                g.tensor_tensor(hp[1][:, s % HR, 0:T], h32[:, s % HR, :], hp[0][:, s % HR, 0:T],
                                ALU.subtract).then_inc(S["lo_done"], 1)

            def gather(f, e):
                for t in range(NT):
                    pool.wait_ge(S["evac_done"], NT * (E * f + e) + t + 2)
                    if e > 0:
                        pool.wait_ge(S["acc_done"], NT * (E * f + e) + t + 1)
                    elif t == 0:
                        pool.wait_ge(S["acc_init"], f + 1)
                    g.tensor_tensor(acc[:, t, :], acc[:, t, :], tmp[:, t, :],
                                    ALU.add).then_inc(S["acc_done"], 1)

            def experts(f, s):
                low(f, s)
                if s == 4:
                    pool.wait_ge(S["out_done"], 16 * f + 16)
                    pool.wait_ge(S["base_ready"], f + 1)
                    pool.sem_inc(S["pool_passed"], 1)
                    g.tensor_copy(acc, h0[:, :, :]).then_inc(S["acc_init"], 1)
                if s % HJ == LAG + 1 and s > HJ:
                    gather(f, s // HJ - 1)

            def weight_scale(t):
                e, kind = t // 2, t % 2
                one = lambda z, k: z[:, k, e:e + 1]
                pool.wait_ge(S["sq_done"], t + 1)
                step(g.partition_all_reduce(one(ssr, kind), one(ssq, kind), 128, RADD))
                step(g.tensor_scalar(one(ssr, kind), one(ssr, kind), WCAP ** -2, 1e-30, ALU.mult, ALU.add))
                step(g.tensor_tensor(one(i_w, kind), one(ssr, kind), exps[:, 1:2], ALU.pow))
                g.tensor_tensor(one(s_w, kind), one(ssr, kind), exps[:, 0:1], ALU.pow).then_inc(S["scale_done"], 1)

            def weight_low(t, half):
                e, kind = t // 2, t % 2
                part_of = slice(half * 1024, half * 1024 + 1024)
                hi, lo = [w[:, e, :, :].rearrange("p a b -> p (a b)")[:, part_of] for w in (w1p if kind == 0 else w2p)]
                if half == 0:
                    pool.wait_ge(S["ws_ready"], t + 1)
                g.tensor_tensor(lo, raw[slot_of(t)[0]][:, part_of], hi, ALU.subtract).then_inc(S["wlo_done"], 1)

            def hidden_scales():
                step(g.partition_all_reduce(ssr[:, 2, :], ssq[:, 2, :], 128, RADD))
                step(g.tensor_scalar(ssr[:, 2, :], ssr[:, 2, :], WCAP ** -2, 1e-30, ALU.mult, ALU.add))
                step(g.tensor_tensor(fb[:, :], ssr[:, 2, :], exps[:, 1:2].broadcast_to([128, E]), ALU.pow))
                step(g.tensor_scalar(ih[:, :], i_w[:, 0, :], 16.0, 1.0, ALU.mult, ALU.mult))
                step(g.tensor_tensor(ih[:, :], ih[:, :], fb[:, :], ALU.add))
                step(g.tensor_tensor(sh[:, :], ih[:, :], exps[:, 2:3].broadcast_to([128, E]), ALU.pow))
                step(g.tensor_tensor(zs[:, :], sh[:, :], i_w[:, 0, :], ALU.mult))
                step(g.tensor_scalar(zs[:, :], zs[:, :], 1.0 / XS, 1.0, ALU.mult, ALU.mult))
                step(g.tensor_tensor(hb_s[:, :, :], b1_s[:, :, :], sh[:, :].unsqueeze(2).broadcast_to([128, E, HJ]),
                                     ALU.mult))
                g.tensor_tensor(dsc[:, :], ih[:, :], i_w[:, 1, :], ALU.mult).then_inc(S["hscale_ready"], 1)

            pool.sem_inc(S["lo_done"], HR)
            pool.sem_inc(S["acc_done"], NT)
            pool.sem_inc(S["out_done"], 16)
            g.memset(ident[:, :], 0.0).then_inc(S["ident_zero"], 1)
            g.memset(nhalf[:, :], -0.5)
            for n, value in enumerate((-0.5, 0.5, -1.0)):
                g.memset(exps[:, n:n + 1], value).then_inc(S["ident_set"], 1)
            pool.wait_ge(S["ident_zero"], 1)
            pool.wait_ge(S["ident_set"], 3)
            g.affine_select(out=ident[:, :], in_=ident[:, :], compare_op=ALU.not_equal, fill=1.0, base=0,
                            pattern=[[-1, 128]], channel_multiplier=1).then_inc(S["ident_ready"], 1)
            pool.wait_ge(S["const_in"], N_CONST)
            g.tensor_tensor(hb_s[:, :, :], b1_s[:, :, :], b1_s[:, :, :], ALU.mult).then_inc(S["b1sq_ready"], 1)
            for j in range(NT):
                for which in range(2):
                    ahead_power(0, j, which)
            for s in range(STEPS):
                mixer(0, s, True)
                if s % 3 == 0 and 2 <= s // 3 < 2 * E + 2:
                    weight_low(s // 3 - 2, 1)
                if s % 3 == 0 and s // 3 < 2 * E:
                    weight_scale(s // 3)
                if s % 3 == 2 and 1 <= s // 3 < 2 * E + 1:
                    weight_low(s // 3 - 1, 0)
            pool.wait_ge(S["ab_done"], 1)
            hidden_scales()
            pool.wait_ge(S["wlo_done"], 4 * E)
            for n in range(2):
                last = g.memset(hp[n][:, :, T:HW], 0.0)
            last.then_inc(S["hpad_zeroed"], 1)

            def both(b, more):
                for s in range(STEPS):
                    mixer(b, s, more)
                    experts(b - 1, s)
                gather(b - 1, E - 1)

            with pool.Fori(1, NB - 1) as i:
                both(i, True)
            both(NB - 1, False)
            for s in range(STEPS):
                experts(NB - 1, s)
            gather(NB - 1, E - 1)


def kernel(**inputs):
    import concourse.bacc as bacc
    from concourse.bass_utils import run_bass_kernel_spmd as run

    def arr(name):
        return np.asarray(inputs[name])

    def channels(a):
        return np.moveaxis(a.reshape(a.shape[0] // 128, 128, -1), 1, 0).reshape(128, -1)

    by_channel = [arr("L0_tok_ln_gamma"), arr("L0_tok_ln_beta"), arr("L0_attn_conv_w").reshape(D, KC),
                  arr("L0_attn_conv_b"), arr("L0_attn_A_log").T, arr("L0_attn_D_param"), arr("L0_ffn_Wg"),
                  arr("L0_ffn_b1").reshape(E * H)]
    given = {
        "x": arr("x"),
        "tok_w": arr("L0_tok_W").T,
        "tok_b": arr("L0_tok_b"),
        "chan": np.concatenate([channels(a) for a in by_channel], axis=1),
        "win": arr("L0_attn_W_in").T,
        "wout": arr("L0_attn_W_out").T,
        "bg": arr("L0_ffn_bg"),
        "w1": arr("L0_ffn_W1"),
        "w2": arr("L0_ffn_W2"),
        "b2": arr("L0_ffn_b2"),
    }
    nc = bacc.Bacc("TRN2", target_bir_lowering=False, num_devices=1)
    arrays, args = {}, []
    for name, a in given.items():
        a = np.ascontiguousarray(a)
        arrays[f"in_{name}"] = a
        args.append(nc.dram_tensor(f"in_{name}", a.shape, mybir.dt.from_np(a.dtype), kind="ExternalInput").ap())
    out = nc.dram_tensor("out_0", (NB, T, D), F32, kind="ExternalOutput").ap()
    build(nc, *args, out)
    r = run(nc, [arrays], core_ids=[0])
    return r.results[0]["out_0"]
```

```python
import numpy as np
import concourse.bass as bass
from concourse import mybir
from contextlib import ExitStack

F32 = mybir.dt.float32
F16 = mybir.dt.float16
BF16 = mybir.dt.bfloat16
ALU = mybir.AluOpType
ACT = mybir.ActivationFunctionType
AX = mybir.AxisListType
RADD = bass.bass_isa.ReduceOp.add

NB = 8
D = 256
RF = 2
T = 375
NT, P = 3, 125
DH = D // 128
FK = D * RF // 128
NS = 32
NP = NS // 2
ROWS = 2 * NS
RR = 3
DR = 3
SL = 3
E = 8
H = 1024
HJ = H // 128
STEPS = E * HJ
KC = 4
EPS = 1e-5

XS = 2.0 ** 11
WCAP = 2.0 ** 14

ZR = 2
HR = 4
LAG = 3
HW = 384
SR = 6
TENSORS = [(e, kind) for e in range(E - 2) for kind in range(2)]
TENSORS += [(e, kind) for kind in range(2) for e in (E - 2, E - 1)]
SLOT = [2, 3, 4, 5, 0, 1] * 2 + [4, 5, 0, 1]

AT_BC = 1
AT_SCAN, SCAN_STEPS = 4, 46
AT_OUT, AT_T2, AT_GATE, AT_WT, AT_B2 = 53, 56, 58, 61, 63
TO_X, TO_TOK, TO_T1 = 3, 6, 4
TO_HIGH, TO_COPY, TO_LOW = 3, 4, (5, 6)


def at_row(k):
    return AT_SCAN + (k * SCAN_STEPS) // ROWS


def at_state(n):
    return AT_SCAN + (n * SCAN_STEPS) // NS


def at_pair(p):
    return AT_SCAN + (p * SCAN_STEPS) // NP


def norm_at(j, which):
    return 5 * j + which * 4


def row(k):
    if k == 0:
        return 0, 0
    if k == ROWS - 1:
        return 1, NS - 1
    return (0, (k + 1) // 2) if k % 2 else (1, k // 2 - 1)


def at_tensor(t):
    return 0 if t == 1 else 1 + (t - 2) * 52 // (2 * E - 2)


ROW_AT = {row(k): k for k in range(ROWS)}


CHAN = {"gamma": (FK,), "beta": (FK,), "conv_w": (DH, KC), "conv_b": (DH,), "a_log": (DH, NS), "d_par": (DH,),
        "wg": (DH, E), "b1": (E, HJ)}


def build(nc, x, tok_w, tok_b, chan, win, wout, bg, w1, w2, b2, out):
    with ExitStack() as ctx:
        def sb(name, shape, dt=F32):
            return ctx.enter_context(nc.sbuf_tensor(name, shape, dt))

        def sem(name):
            return ctx.enter_context(nc.semaphore(name))

        ident = sb("ident", [128, 128])
        pick = sb("pick", [96, NS], BF16)
        tokw_s = sb("tokw_s", [128, FK, D])
        win_s = sb("win_s", [128, DH, 2 * D])
        wbc_s = sb("wbc_s", [128, DH, 2, 3, NS])
        wout_s = sb("wout_s", [128, DH, D])
        chan_s = sb("chan_s", [128, chan.shape[1]])
        view, at = {}, 0
        for name, dims in CHAN.items():
            width = int(np.prod(dims))
            view[name] = chan_s[:, at:at + width]
            if len(dims) > 1:
                view[name] = view[name].rearrange("p (a b) -> p a b", a=dims[0])
            at += width
        gam_s, bet_s, cw_s, cb_s, a_s, d_s, wg_s, b1_s = view.values()
        bg_s = sb("bg_s", [P, E])
        row_s = sb("row_s", [33, D])
        b2_s = row_s[0:E, :]
        tokb_s = row_s[32:33, :]
        one = ident[32:33, 32:33]
        w1p = [sb(f"w1_{p}", [128, E, DH, H], F16) for p in ("hi", "lo")]
        w2p = [sb(f"w2_{p}", [128, E, HJ, D], F16) for p in ("hi", "lo")]

        ssq = sb("ssq", [128, 3, E])
        ssr = sb("ssr", [128, 3, E])
        s_w = sb("s_w", [128, 2, E])
        i_w = sb("i_w", [128, 2, E])
        fb = sb("fb", [128, E])
        ih = sb("ih", [128, E])
        sh = sb("sh", [128, E])
        zs = sb("zs", [128, E])
        hb_s = sb("hb_s", [128, E, HJ])
        dsc = sb("dsc", [128, E])
        exps = sb("exps", [128, 3])
        nhalf = sb("nhalf", [P, NT])

        decay = sb("decay", [128, DR, DH, T])
        hs = sb("hs", [128, SL, DH, T])
        y = sb("y", [128, DH, T])
        up0 = sb("up0", [128, DH, T + KC - 1])
        part = up0[:, :, KC - 1:]
        u = sb("u", [128, DH, T])
        dl = sb("dl", [128, DH, T])
        h0 = sb("h0", [P, NT, D])
        bct = hs[0:96, 0, :, :]
        bcm = hs[0:96, 1, 0, :].bitcast(BF16).rearrange("p (k t) -> p k t", k=2)
        xh = hs[0:P, 0:2, :, :].rearrange("p s h t -> p (s h t)")[:, 0:NT * D].rearrange("p (j c) -> p j c", j=NT)
        xT2 = hs[:, 2, :, :]
        x_tok = sb("x_tok", [P, D * RF])
        xT0_s = sb("xT0", [128, FK * P])
        h0n = sb("h0n", [P, NT, D])
        xT1 = sb("xT1", [128, DH, T])
        stn = sb("stn", [P, 2, 6])
        mvn = sb("mvn", [P, 2, 2])
        ven = sb("ven", [P, 2])
        rsn = sb("rsn", [P, 2])
        bcf = sb("bcf", [96, T])
        bcs = bcf[:, :].bitcast(BF16).rearrange("p (g t) -> p g t", g=2)
        st = sb("st", [P, NT, 6])
        mv = sb("mv", [P, NT, 2])
        ve = sb("ve", [P, NT])
        rs = sb("rs", [P, NT])
        gz = sb("gz", [P, NT, E])
        gw = sb("gw", [P, NT, E])
        gwt = bcf[0:E, :]
        gsc = sb("gsc", [P, NT, E])

        FA = HR * T + NT * D + NT * D + 2 * T + HR * HW
        fa = sb("fa", [128, FA])
        raw = [fa[:, 2048 * n:2048 * (n + 1)] for n in range(2)]
        raw += [w[:, E - 2:E, :, :].rearrange("p e a b -> p (e a b)").bitcast(F32) for w in w1p + w2p]
        assert len(raw) == SR
        h32 = fa[:, 0:HR * T].rearrange("p (r t) -> p r t", r=HR)
        o = HR * T
        acc = fa[0:P, o:o + NT * D].rearrange("p (j c) -> p j c", j=NT)
        o += NT * D
        tmp = fa[0:P, o:o + NT * D].rearrange("p (j c) -> p j c", j=NT)
        o += NT * D
        x2 = [fa[:, o + n * T:o + (n + 1) * T].bitcast(F16).rearrange("p (h t) -> p h t", h=DH)
              for n in range(2)]
        o += 2 * T
        hp = [fa[:, o + n * HR * HW // 2:o + (n + 1) * HR * HW // 2].bitcast(F16).rearrange(
            "p (r t) -> p r t", r=HR) for n in range(2)]
        o += HR * HW
        assert o == FA and FA >= 2 * 2048
        gcur = sb("gcur", [P, NT, E])

        M = ctx.enter_context(nc.psum_tensor("M", [128, 4, 512], F32))
        Z = ctx.enter_context(nc.psum_tensor("Z", [128, ZR, 512], F32))
        O = ctx.enter_context(nc.psum_tensor("O", [128, 2, 512], F32))

        def place(b, j):
            if isinstance(b, int) and b == 0:
                rows_in = (x_tok[:, :], u[0:P, :, :].rearrange("p h t -> p (h t)")[:, 0:RF * D],
                           dl[0:P, :, :].rearrange("p h t -> p (h t)")[:, 0:RF * D])[j]
                return rows_in, hs[:, j, :, :].rearrange("p h t -> p (h t)")[:, 0:FK * P], M[:, 1 + j, :]
            return x_tok[:, :], xT0_s[:, :], M[:, RR, :]

        def low_done(n):
            return 2 * (n - 1)

        def before(t):
            return max((n + 1 for n in range(t) if SLOT[n] == SLOT[t]), default=0)

        def rows(tile):
            return tile // 2, slice((tile % 2) * D, (tile % 2) * D + D)

        names = """const_in tok_in ident_zero ident_set ident_ready a_exp a_ready_neg b1sq_ready pool_step
            x_in var_ready rstd_ready xhat0_ready xhat1_ready xhat2_ready xT0_psum xT0_ready a_cleared
            ahead_step xvar_ready xrstd_ready hvar_ready hrstd_ready h0n_ready beta_psum tokb_ready tokw_ready
            tok_psum h0_ready xT1_psum xT1_ready u_psum u_padded pad_zeroed delta_psum sp_ready delta_ready bc_psum
            bchi_ready bcs_ready decay_ready row_ready row_used scan_done part_ready y_added y_ready
            out_psum xT2_psum xT2_ready gate_psum gz_ready ge_ready gw_ready gwt_psum gwt_ready b2_psum
            base_ready gsc_ready x2hi_ready x2lo_ready gcur_ready act_step dve_step hpad_zeroed
            z_ready relu_done lo_done mm2_done evac_done acc_done acc_init out_done
            sq_done scale_done whi_ready ws_ready wlo_done wlo_first hscale_ready ab_done dve_passed pool_passed""".split()
        S = {n: sem(n) for n in names}
        raw_in = [sem(f"raw_in{n}") for n in range(SR)]

        block = ctx.enter_context(nc.Block())

        x_v = x.rearrange("b (j p r) c -> b j p (r c)", j=NT, p=P, r=RF)
        out_v = out.rearrange("b (j p) c -> b p j c", j=NT, p=P)

        def wait(eng, name, value):
            if not isinstance(value, int) or value > 0:
                eng.wait_ge(S[name], value)

        consts = [(chan_s, chan),
                  (tokw_s, tok_w.rearrange("(k p) n -> p k n", p=128)),
                  (tokb_s, tok_b.unsqueeze(0)),
                  (win_s, win[:, 0:2 * D].rearrange("(k p) n -> p k n", p=128)),
                  (wout_s, wout.rearrange("(k p) n -> p k n", p=128)),
                  (bg_s, bg.partition_broadcast(P)),
                  (b2_s, b2)]
        wbc_v = win[:, 2 * D:2 * D + 2 * NS].rearrange("(k p) (g n) -> p k g n", p=128, g=2)
        N_TOK = 16 * 3
        N_CONST = 16 * (len(consts) + 6) - N_TOK

        @block.sync
        def _(sp):
            def load_x(b, j):
                if not (isinstance(b, int) and b == 0):
                    sp.wait_ge(S["xT0_psum"], NT * b + j)
                sp.dma_start(place(b, j)[0], x_v[b, j]).then_inc(S["x_in"], 16)

            def load_weights(t):
                if before(t) == 1:
                    sp.wait_ge(S["wlo_first"], 1)
                elif before(t) > 1:
                    sp.wait_ge(S["wlo_done"], low_done(before(t)))
                e, kind = TENSORS[t]
                src = w2[e].rearrange("(j p) n -> p j n", p=128) if kind else w1[e].rearrange("(k p) n -> p k n", p=128)
                dst = raw[SLOT[t]].rearrange("p (k n) -> p k n", k=HJ if kind else DH)
                sp.dma_start(dst, src).then_inc(raw_in[SLOT[t]], 16)

            def store(b):
                sp.wait_ge(S["acc_done"], NT * E * (b + 1) + NT)
                sp.dma_start(out_v[b], acc).then_inc(S["out_done"], 16)

            for j in range(NT):
                load_x(0, j)
            for n, (dst, src) in enumerate(consts):
                sp.dma_start(dst[tuple(slice(None) for _ in dst.shape)], src).then_inc(
                    S["tok_in" if n < N_TOK // 16 else "const_in"], 16)
                if n == N_TOK // 16:
                    load_weights(0)
            for r in range(3):
                for g in range(2):
                    sp.dma_start(wbc_s[:, :, g, r, :], wbc_v[:, :, g, :]).then_inc(S["const_in"], 16)
            load_weights(1)
            load_x(1, 0)
            for t in range(2, 2 * E):
                load_weights(t)
                if t == 7:
                    load_x(1, 1)
                if t == 11:
                    load_x(1, 2)
            with sp.Fori(1, NB - 1) as i:
                for j in range(NT):
                    load_x(i + 1, j)
                store(i - 1)
            store(NB - 2)
            store(NB - 1)
            sp.wait_ge(S["out_done"], 16 * (NB + 1))

        @block.tensor
        def _(pe):
            mm = nc.tensor.matmul

            def transposes(dst, src, k, width):
                for j in range(NT):
                    last = nc.tensor.transpose(dst[0:width, j * P:(j + 1) * P],
                                               src[:, j, k * 128:k * 128 + width], ident[0:P, 0:P])
                return last

            def token_major(name, src, parts, w, bank):
                for j in range(NT):
                    b, cols = rows(j)
                    for k in range(parts):
                        last = mm(M[0:P, bank + b, cols], src[:, k, j * P:(j + 1) * P], w[:, k, :],
                                  start=(k == 0), stop=(k == parts - 1))
                    if j > 0:
                        last.then_inc(S[name], 1)

            def turn_x(b, j):
                pe.wait_ge(S["xhat0_ready"], NT * b + j + 1)
                x_rows, _, bank = place(b, j)
                if not (isinstance(b, int) and b == 0):
                    pe.wait_ge(S["xT1_ready"], NT * b + j)
                for k in range(FK):
                    last = nc.tensor.transpose(bank[:, k * P:(k + 1) * P], x_rows[:, k * 128:(k + 1) * 128],
                                               ident[0:P, 0:P])
                last.then_inc(S["xT0_psum"], 1)

            def tokens(b, j):
                _, turned, bank = place(b, j)
                pe.wait_ge(S["xT0_ready"], NT * b + j + 1)
                mm(bank[0:P, 0:D], one.broadcast_to([1, P]), tokb_s, start=True, stop=False)
                for k in range(FK):
                    last = mm(bank[0:P, 0:D], turned[:, k * P:(k + 1) * P], tokw_s[:, k, :], start=False,
                              stop=(k == FK - 1))
                last.then_inc(S["tok_psum"], 1)

            def turn_tokens(b, j):
                _, turned, bank = place(b, j)
                pe.wait_ge(S["xhat1_ready"], NT * b + j + 1)
                for h in range(DH):
                    last = nc.tensor.transpose(bank[:, D + h * P:D + (h + 1) * P],
                                               turned[0:P, h * 128:(h + 1) * 128], ident[0:P, 0:P])
                last.then_inc(S["xT1_psum"], 1)

            def ahead(b, s):
                for j in range(NT):
                    if s == at_pair(norm_at(j, 0) + 1) + TO_X:
                        turn_x(b + 1, j)
                    if s == at_pair(norm_at(j, 0) + 1) + TO_TOK:
                        tokens(b + 1, j)
                    if s == at_pair(norm_at(j, 1) + 1) + TO_T1:
                        turn_tokens(b + 1, j)

            def mixer(b, s, more):
                if s == 0:
                    pe.wait_ge(S["xT1_ready"], NT * b + NT)
                    wait(pe, "base_ready", b)
                    project("u_psum", 0, 0)
                    project("delta_psum", D, 2)
                if s == AT_BC:
                    pe.wait_ge(S["u_padded"], b + 1)
                    for g in range(2):
                        for k in range(DH):
                            last = mm(M[0:96, g, 0:T], wbc_s[:, k, g, :, :].rearrange("p r n -> p (r n)"),
                                      xT1[:, k, :], start=(k == 0), stop=(k == DH - 1))
                    last.then_inc(S["bc_psum"], 1)
                for k in range(ROWS):
                    if s == at_row(k):
                        spread(b, k)
                if more:
                    ahead(b, s)
                if s == AT_OUT:
                    pe.wait_ge(S["y_ready"], b + 1)
                    token_major("out_psum", y, DH, wout_s, 0)
                if s == AT_T2:
                    pe.wait_ge(S["xhat2_ready"], b + 1)
                    if more:
                        pe.wait_ge(S["xT1_ready"], NT * b + 2 * NT)
                    for h in range(DH):
                        last = transposes(M[:, 2 + h, :], xh, h, 128)
                    last.then_inc(S["xT2_psum"], 1)
                if s == AT_GATE:
                    pe.wait_ge(S["xT2_ready"], b + 1)
                    for j in range(NT):
                        for k in range(DH):
                            last = mm(M[0:P, 0, j * E:(j + 1) * E], xT2[:, k, j * P:(j + 1) * P], wg_s[:, k, :],
                                      start=(k == 0), stop=(k == DH - 1))
                    last.then_inc(S["gate_psum"], 1)
                if s == AT_WT:
                    pe.wait_ge(S["gw_ready"], b + 1)
                    transposes(M[:, 1, :], gw, 0, E).then_inc(S["gwt_psum"], 1)
                if s == AT_B2:
                    pe.wait_ge(S["gwt_ready"], b + 1)
                    for j in range(NT):
                        bk, cols = rows(j)
                        last = mm(M[0:P, 2 + bk, cols], gwt[:, j * P:(j + 1) * P], b2_s[:, :], start=True, stop=True)
                    last.then_inc(S["b2_psum"], 1)

            def project(name, col, bank):
                for h in range(DH):
                    for k in range(DH):
                        last = mm(M[:, bank + h, 0:T], win_s[:, k, col + h * 128:col + (h + 1) * 128],
                                  xT1[:, k, :], start=(k == 0), stop=(k == DH - 1))
                last.then_inc(S[name], 1)

            def spread(b, k):
                g, n = row(k)
                if k == 0:
                    pe.wait_ge(S["bcs_ready"], b + 1)
                if k == 2:
                    pe.wait_ge(S["delta_ready"], b + 1)
                if k >= RR:
                    pe.wait_ge(S["row_used"], ROWS * b + k - RR + 1)
                mm(M[:, k % RR, 0:T], pick[:, n:n + 1].broadcast_to([96, 128]), bcs[:, g, :],
                   start=True, stop=True).then_inc(S["row_ready"], 1)

            def first(f, s):
                e, j = s // HJ, s % HJ
                pe.wait_ge(S["relu_done"], STEPS * f + s + 1)
                n = 0
                for k in range(DH):
                    for wp, xp in ((0, 0), (0, 1), (1, 0)):
                        n += 1
                        last = mm(Z[:, s % ZR, 0:T], w1p[wp][:, e, k, j * 128:(j + 1) * 128], x2[xp][:, k, :],
                                  start=(n == 1), stop=(n == 3 * DH))
                last.then_inc(S["z_ready"], 1)

            def second(f, s):
                e, j = s // HJ, s % HJ
                if j == 0:
                    pe.wait_ge(S["evac_done"], NT * (E * f + e) + 1)
                pe.wait_ge(S["lo_done"], STEPS * f + s + 1 + HR)
                for t in range(NT):
                    b, cols = rows(t)
                    for n, (hq, wp) in enumerate(((0, 0), (0, 1), (1, 0))):
                        last = mm(O[:, b, cols], hp[hq][:, s % HR, t * P:t * P + 128], w2p[wp][:, e, j, :],
                                  start=(j == 0 and n == 0 and t != 1), stop=(j == HJ - 1 and n == 2),
                                  skip_group_check=True)
                last.then_inc(S["mm2_done"], 1)

            def experts(f, s):
                first(f, s)
                if s < LAG:
                    return
                if s % HJ == LAG and s > HJ:
                    return
                if s % HJ == LAG + 1 and s > HJ:
                    second(f, s - LAG - 1)
                second(f, s - LAG)

            def tail(f):
                for s in range(STEPS - LAG, STEPS):
                    second(f, s)

            pe.sem_inc(S["mm2_done"], HR)
            pe.wait_ge(S["ident_ready"], 1)
            pe.wait_ge(S["tok_in"], N_TOK)
            for k in range(FK):
                mm(M[0:1, 0, 0:D], bet_s[:, k:k + 1], tokw_s[:, k, :], start=(k == 0), stop=False)
            mm(M[0:1, 0, 0:D], one, tokb_s, start=False, stop=True).then_inc(S["beta_psum"], 1)
            for j in range(NT):
                turn_x(0, j)
            pe.wait_ge(S["tokb_ready"], 1)
            pe.wait_ge(S["tokw_ready"], 1)
            for j in range(NT):
                tokens(0, j)
            for j in range(NT):
                turn_tokens(0, j)
            pe.wait_ge(S["const_in"], N_CONST)
            for s in range(STEPS):
                mixer(0, s, True)

            def both(b, more):
                mixer(b, 0, more)
                pe.wait_ge(S["x2lo_ready"], b)
                experts(b - 1, 0)
                for s in range(1, STEPS):
                    mixer(b, s, more)
                    experts(b - 1, s)
                tail(b - 1)

            with pe.Fori(1, NB - 1) as i:
                both(i, True)
            both(NB - 1, False)
            pe.wait_ge(S["x2lo_ready"], NB)
            for s in range(STEPS):
                experts(NB - 1, s)
            tail(NB - 1)

        @block.scalar
        def _(act):
            fn = nc.scalar.activation
            ACT_STEPS = 2
            AT_H0 = AT_SCAN + 4

            def input_turned(b, j):
                act.wait_ge(S["xT0_psum"], NT * b + j + 1)
                fn(place(b, j)[1], place(b, j)[2][:, 0:FK * P], ACT.Copy).then_inc(S["xT0_ready"], 1)

            def token_rows(b, j):
                act.wait_ge(S["tok_psum"], NT * b + j + 1)
                wait(act, "h0_ready", b)
                fn(h0n[:, j, :], place(b, j)[2][0:P, 0:D], ACT.Relu).then_inc(S["h0n_ready"], 1)

            def tokens_turned(b, j):
                act.wait_ge(S["xT1_psum"], NT * b + j + 1)
                wait(act, "bc_psum", b)
                fn(xT1[:, :, j * P:(j + 1) * P], place(b, j)[2][:, D:D + DH * P].rearrange("p (h t) -> p h t", h=DH),
                   ACT.Copy).then_inc(S["xT1_ready"], 1)

            def ahead(b, s):
                for j in range(NT):
                    if s == at_pair(norm_at(j, 0) + 1) + TO_X + 1:
                        input_turned(b + 1, j)
                    if s == at_pair(norm_at(j, 0) + 1) + TO_TOK + 1:
                        token_rows(b + 1, j)
                    if s == at_pair(norm_at(j, 1) + 1) + TO_T1 + 1:
                        tokens_turned(b + 1, j)

            def mixer(b, s, more):
                if s == 0:
                    act.wait_ge(S["u_psum"], b + 1)
                    fn(up0[:, :, KC - 1:], M[:, 0:2, 0:T], ACT.Copy).then_inc(S["u_padded"], 1)
                    act.wait_ge(S["delta_psum"], b + 1)
                    fn(dl[:, :, :], M[:, 2:4, 0:T], ACT.Abs).then_inc(S["act_step"], 1)
                    act.wait_ge(S["act_step"], ACT_STEPS * b + 1)
                    fn(dl[:, :, :], dl[:, :, :], ACT.Exp, scale=-1.0).then_inc(S["act_step"], 1)
                    act.wait_ge(S["act_step"], ACT_STEPS * b + 2)
                    fn(dl[:, :, :], dl[:, :, :], ACT.Ln, bias=1.0).then_inc(S["sp_ready"], 1)
                if s == AT_BC:
                    act.wait_ge(S["bc_psum"], b + 1)
                    fn(bcs[:, :, :], M[0:96, 0:2, 0:T], ACT.Copy).then_inc(S["bchi_ready"], 1)
                for n in range(NS):
                    if s == max(at_state(n) - 1, AT_BC):
                        if n == 0:
                            if isinstance(b, int) and b == 0:
                                act.wait_ge(S["a_ready_neg"], 1)
                            act.wait_ge(S["delta_ready"], b + 1)
                            act.wait_ge(S["a_cleared"], 1)
                        if n >= DR:
                            act.wait_ge(S["scan_done"], NS * b + n - DR + 1)
                        for h in range(DH):
                            last = fn(decay[:, n % DR, h, 1:T], dl[:, h, 1:T], ACT.Exp, scale=a_s[:, h, n:n + 1])
                        last.then_inc(S["decay_ready"], 1)
                if s == AT_H0:
                    act.wait_ge(S["h0n_ready"], NT * b + NT)
                    wait(act, "acc_init", b)
                    fn(h0[:, :, :], h0n[:, :, :], ACT.Copy).then_inc(S["h0_ready"], 1)
                if more:
                    ahead(b, s)
                if s == AT_T2 + 1:
                    act.wait_ge(S["xT2_psum"], b + 1)
                    fn(xT2[:, :, :], M[:, 2:4, 0:T], ACT.Copy, scale=XS).then_inc(S["xT2_ready"], 1)
                if s == AT_GATE + 1:
                    act.wait_ge(S["gz_ready"], b + 1)
                    fn(gz[:, :, :], gz[:, :, :], ACT.Exp, scale=-1.0).then_inc(S["ge_ready"], 1)

            def next_rows(b):
                wait(act, "z_ready", STEPS * b)
                act.wait_ge(S["xT2_ready"], b + 1)
                fn(x2[0], xT2[:, :, :], ACT.Copy).then_inc(S["x2hi_ready"], 1)

            def next_gates(b):
                act.wait_ge(S["evac_done"], NT * E * b + 1)
                act.wait_ge(S["gsc_ready"], b + 1)
                fn(gcur[:, :, :], gsc[:, :, :], ACT.Copy).then_inc(S["gcur_ready"], 1)

            def relu(f, s):
                e, j = s // HJ, s % HJ
                act.wait_ge(S["z_ready"], STEPS * f + s + 1)
                act.wait_ge(S["lo_done"], STEPS * f + s + 1)
                args = dict(bias=hb_s[:, e, j:j + 1], scale=zs[:, e:e + 1])
                fn(h32[:, s % HR, :], Z[:, s % ZR, 0:T], ACT.Relu, **args)
                act.wait_ge(S["mm2_done"], STEPS * f + s + 1)
                fn(hp[0][:, s % HR, 0:T], Z[:, s % ZR, 0:T], ACT.Relu, **args).then_inc(S["relu_done"], 1)

            def evacuate(f, e):
                act.wait_ge(S["mm2_done"], STEPS * f + HJ * (e + 1) + HR)
                act.wait_ge(S["gcur_ready"], f + 1)
                for t in range(NT):
                    b, cols = rows(t)
                    act.wait_ge(S["acc_done"], NT * (E * f + e) + t + 1)
                    fn(tmp[:, t, :], O[0:P, b, cols], ACT.Copy,
                       scale=gcur[:, t, e:e + 1]).then_inc(S["evac_done"], 1)

            def experts(f, s):
                relu(f, s)
                if s % HJ == LAG - 1 and s > HJ:
                    evacuate(f, s // HJ - 1)

            def square_weights(t):
                e, kind = TENSORS[t]
                hi = (w1p if kind == 0 else w2p)[0][:, e, :, :].rearrange("p a b -> p (a b)")
                act.wait_ge(raw_in[SLOT[t]], 16 * SLOT[:t + 1].count(SLOT[t]))
                if e >= E - 2:
                    act.wait_ge(S["wlo_done"], low_done(max(n for n in range(2 * E) if SLOT[n] == 2 + 2 * kind) + 1))
                fn(hi, raw[SLOT[t]], ACT.Square, accum_out=ssq[:, kind, e:e + 1]).then_inc(S["sq_done"], 1)

            def weight_high(t):
                e, kind = TENSORS[t]
                hi = (w1p if kind == 0 else w2p)[0][:, e, :, :].rearrange("p a b -> p (a b)")
                act.wait_ge(S["scale_done"], t + 1)
                fn(hi, raw[SLOT[t]], ACT.Copy, scale=s_w[:, kind, e:e + 1]).then_inc(S["whi_ready"], 1)

            def scale_weights(t):
                e, kind = TENSORS[t]
                r = raw[SLOT[t]]
                act.wait_ge(S["whi_ready"], t + 1)
                fn(r, r, ACT.Copy, scale=s_w[:, kind, e:e + 1]).then_inc(S["ws_ready"], 1)

            def prepare(s):
                for t in range(1, 2 * E):
                    if s == at_tensor(t) and t > 1:
                        square_weights(t)
                    if s == at_tensor(t) + TO_HIGH:
                        weight_high(t)
                    if s == at_tensor(t) + TO_COPY:
                        scale_weights(t)

            nc.scalar.preload_act_table_set("natural_log_exp_and_others")
            act.sem_inc(S["relu_done"], ZR)
            act.sem_inc(S["evac_done"], 1)
            act.wait_ge(S["tok_in"], N_TOK)
            fn(a_s[:, :, :], a_s[:, :, :], ACT.Exp).then_inc(S["a_exp"], 1)
            act.wait_ge(S["a_exp"], 1)
            fn(a_s[:, :, :], a_s[:, :, :], ACT.Copy, scale=-1.0).then_inc(S["a_ready_neg"], 1)
            for j in range(NT):
                input_turned(0, j)
            for j in range(NT):
                token_rows(0, j)
            square_weights(0)
            for j in range(NT):
                tokens_turned(0, j)
            weight_high(0)
            square_weights(1)
            for s in range(STEPS):
                mixer(0, s, True)
                prepare(s)
            act.wait_ge(S["wlo_done"], low_done(2 * E))
            next_rows(0)
            next_gates(0)
            act.wait_ge(S["hscale_ready"], 1)
            act.wait_ge(S["hpad_zeroed"], 1)

            def both(b, more):
                for s in range(STEPS):
                    mixer(b, s, more)
                    experts(b - 1, s)
                next_rows(b)
                evacuate(b - 1, E - 1)
                next_gates(b)

            with act.Fori(1, NB - 1) as i:
                both(i, True)
            both(NB - 1, False)
            for s in range(STEPS):
                experts(NB - 1, s)
            evacuate(NB - 1, E - 1)

        @block.vector
        def _(dve):
            v = nc.vector
            per_batch = {}

            NORM = ({"variance": "xvar_ready", "rstd": "xrstd_ready", "rows": "xhat0_ready"},
                    {"variance": "hvar_ready", "rstd": "hrstd_ready", "rows": "xhat1_ready"})

            def stats(b, j, which):
                if which == 0:
                    dve.wait_ge(S["x_in"], 16 * (NT * b + j + 1))
                else:
                    dve.wait_ge(S["h0n_ready"], NT * b + j + 1)
                v.bn_stats(stn[:, which, :], x_tok[:, :] if which == 0 else h0n[:, j, :]).then_inc(S["ahead_step"], 1)

            def moments(b, j, which):
                wait(dve, NORM[which]["rows"], NT * b + j)
                dve.wait_ge(S["ahead_step"], 4 * (NT * b + j) + 2 * which + 1)
                dve.sem_inc(S["dve_passed"], 1)
                v.bn_aggr(mvn[:, which, :], stn[:, which, :]).then_inc(S["ahead_step"], 1)

            def variance(b, j, which):
                dve.wait_ge(S["ahead_step"], 4 * (NT * b + j) + 2 * which + 2)
                v.tensor_scalar(ven[:, which:which + 1], mvn[:, which, 1:2], EPS, None,
                                ALU.add).then_inc(S[NORM[which]["variance"]], 1)

            def normalise(b, j, which):
                dve.wait_ge(S[NORM[which]["rstd"]], NT * b + j + 1)
                src, dst = (x_tok[:, :], x_tok[:, :]) if which == 0 else (h0n[:, j, :], xT0_s[0:P, 0:D])
                v.tensor_scalar(dst, src, mvn[:, which, 0:1], rsn[:, which:which + 1],
                                ALU.subtract, ALU.mult).then_inc(S[NORM[which]["rows"]], 1)

            def first_norm(which):
                for j in range(NT):
                    if which:
                        dve.wait_ge(S["h0n_ready"], j + 1)
                    elif j == 0:
                        dve.wait_ge(S["x_in"], 16 * NT)
                    v.bn_stats(st[:, j, :], h0n[:, j, :] if which else place(0, j)[0]).then_inc(S["ahead_step"], 1)
                dve.wait_ge(S["ahead_step"], 2 * NT * which + NT)
                if which:
                    dve.wait_ge(S["xhat0_ready"], NT)
                for j in range(NT):
                    v.bn_aggr(mv[:, j, :], st[:, j, :]).then_inc(S["ahead_step"], 1)
                dve.wait_ge(S["ahead_step"], 2 * NT * which + 2 * NT)
                v.tensor_scalar(ve[:, :], mv[:, :, 1], EPS, None, ALU.add).then_inc(S[NORM[which]["variance"]], NT)
                dve.wait_ge(S[NORM[which]["rstd"]], NT)
                for j in range(NT):
                    src, dst = (h0n[:, j, :], place(0, j)[1][0:P, 0:D]) if which else [place(0, j)[0]] * 2
                    v.tensor_scalar(dst, src, mv[:, j, 0:1], rs[:, j:j + 1], ALU.subtract,
                                    ALU.mult).then_inc(S[NORM[which]["rows"]], 1)

            def batch(b, more):
                count = [0]
                base = 0 if isinstance(b, int) and b == 0 else b * per_batch["steps"]

                def step(ins):
                    ins.then_inc(S["dve_step"], 1)
                    count[0] += 1
                    return count[0]

                def done(n):
                    dve.wait_ge(S["dve_step"], base + n)

                def norm(src, dst, name):
                    for j in range(NT):
                        n = step(v.bn_stats(st[:, j, :], src[:, j, :]))
                    done(n)
                    dve.sem_inc(S["dve_passed"], 1)
                    for j in range(NT):
                        n = step(v.bn_aggr(mv[:, j, :], st[:, j, :]))
                    done(n)
                    v.tensor_scalar(ve[:, :], mv[:, :, 1], EPS, None, ALU.add).then_inc(S["var_ready"], 1)
                    dve.wait_ge(S["rstd_ready"], b + 1)
                    for j in range(NT):
                        last = v.tensor_scalar(dst[:, j, :], src[:, j, :], mv[:, j, 0:1], rs[:, j:j + 1],
                                               ALU.subtract, ALU.mult)
                    last.then_inc(S[name], 1)

                dve.wait_ge(S["u_padded"], b + 1)
                if isinstance(b, int) and b == 0:
                    dve.wait_ge(S["pad_zeroed"], 1)
                wait(dve, "x2lo_ready", b)
                for k in range(KC):
                    if k:
                        done(n)
                    for h in range(DH):
                        if k == 0:
                            n = step(v.tensor_scalar(u[:, h, :], up0[:, h, 0:T], cw_s[:, h, 0:1], cb_s[:, h:h + 1],
                                                     ALU.mult, ALU.add))
                        else:
                            n = step(v.scalar_tensor_tensor(out=u[:, h, :], in0=up0[:, h, k:k + T],
                                                            scalar=cw_s[:, h, k:k + 1], in1=u[:, h, :],
                                                            op0=ALU.mult, op1=ALU.add))
                u_done = n
                dve.wait_ge(S["sp_ready"], b + 1)
                v.scalar_tensor_tensor(out=dl[:, :, :], in0=M[:, 2:4, 0:T], scalar=0.0, in1=dl[:, :, :],
                                       op0=ALU.max, op1=ALU.add).then_inc(S["delta_ready"], 1)
                dve.wait_ge(S["bchi_ready"], b + 1)
                n = step(v.tensor_tensor(bct, M[0:96, 0:2, 0:T], bcs[:, :, :], ALU.subtract))
                done(n)
                n = step(v.tensor_copy(bcm, bct))
                done(n)
                n = step(v.tensor_copy(bcs[32:64, :, :], bcm[32:64]))
                n = step(v.tensor_tensor(bct, bct, bcm, ALU.subtract))
                done(n)
                v.tensor_copy(bcs[64:96, :, :], bct[64:96]).then_inc(S["bcs_ready"], 1)
                dve.wait_ge(S["bcs_ready"], b + 1)
                done(u_done)

                def drive(n):
                    k = ROW_AT[0, n]
                    dve.wait_ge(S["row_ready"], ROWS * b + k + 1)
                    if n >= SL:
                        dve.wait_ge(S["part_ready"], NP * b + (n - SL) // 2 + 1)
                    v.tensor_tensor(hs[:, n % SL, :, :], u[:, :, :],
                                    M[:, k % RR, 0:T].unsqueeze(1).broadcast_to([128, DH, T]),
                                    ALU.mult).then_inc(S["row_used"], 1)

                def scan(n):
                    dve.wait_ge(S["row_used"], ROWS * b + ROW_AT[0, n] + 1)
                    dve.wait_ge(S["decay_ready"], NS * b + n + 1)
                    flat = hs[:, n % SL, :, :].rearrange("p h t -> p (h t)")
                    v.tensor_tensor_scan(flat, decay[:, n % DR, :, :].rearrange("p h t -> p (h t)"), flat,
                                         0.0, ALU.mult, ALU.add).then_inc(S["scan_done"], 1)

                def weigh(n):
                    k = ROW_AT[1, n]
                    dve.wait_ge(S["row_ready"], ROWS * b + k + 1)
                    dve.wait_ge(S["scan_done"], NS * b + n + 1)
                    v.tensor_tensor(hs[:, n % SL, :, :], hs[:, n % SL, :, :],
                                    M[:, k % RR, 0:T].unsqueeze(1).broadcast_to([128, DH, T]),
                                    ALU.mult).then_inc(S["row_used"], 1)

                def pair_sum(p):
                    dve.wait_ge(S["row_used"], ROWS * b + ROW_AT[1, 2 * p + 1] + 1)
                    if p > 1:
                        dve.wait_ge(S["y_added"], (NP - 1) * b + p - 1)
                    v.tensor_tensor(y[:, :, :] if p == 0 else part, hs[:, 2 * p % SL, :, :],
                                    hs[:, (2 * p + 1) % SL, :, :], ALU.add).then_inc(S["part_ready"], 1)

                drive(0)
                scan(0)
                for p in range(NP):
                    now = [(j, which) for j in range(NT) for which in range(2) if more and p == norm_at(j, which)]
                    old = [(j, which) for j in range(NT) for which in range(2) if more and p == norm_at(j, which) + 1]
                    for j, which in old:
                        normalise(b + 1, j, which)
                    drive(2 * p + 1)
                    for j, which in now:
                        stats(b + 1, j, which)
                    weigh(2 * p)
                    scan(2 * p + 1)
                    for j, which in now:
                        moments(b + 1, j, which)
                    if p < NP - 1:
                        drive(2 * p + 2)
                    weigh(2 * p + 1)
                    for j, which in now:
                        variance(b + 1, j, which)
                    if p < NP - 1:
                        scan(2 * p + 2)
                    pair_sum(p)
                dve.wait_ge(S["y_added"], (NP - 1) * (b + 1))
                for h in range(DH):
                    last = v.scalar_tensor_tensor(out=y[:, h, :], in0=u[:, h, :], scalar=d_s[:, h:h + 1],
                                                  in1=y[:, h, :], op0=ALU.mult, op1=ALU.add)
                last.then_inc(S["y_ready"], 1)
                dve.wait_ge(S["h0_ready"], b + 1)
                for j0, w in ((0, 2), (2, 1)):
                    dve.wait_ge(S["out_psum"], 2 * b + 1 + j0 // 2)
                    src = M[0:P, j0 // 2, 0:w * D].rearrange("p (j c) -> p j c", j=w)
                    n = step(v.tensor_tensor(h0[:, j0:j0 + w, :], src, h0[:, j0:j0 + w, :], ALU.add))
                done(n)
                norm(h0, xh, "xhat2_ready")
                dve.wait_ge(S["gate_psum"], b + 1)
                gp = M[0:P, 0, 0:NT * E].rearrange("p (j e) -> p j e", j=NT)
                v.scalar_tensor_tensor(out=gz[:, :, :], in0=gp, scalar=1.0 / XS,
                                       in1=bg_s[:, :].unsqueeze(1).broadcast_to([P, NT, E]),
                                       op0=ALU.mult, op1=ALU.add).then_inc(S["gz_ready"], 1)
                dve.wait_ge(S["ge_ready"], b + 1)
                done(step(v.tensor_scalar(gz[:, :, :], gz[:, :, :], 1.0, None, ALU.add)))
                done(step(v.reciprocal(gz[:, :, :], gz[:, :, :])))
                v.scalar_tensor_tensor(out=gw[:, :, :], in0=gz[:, :, :], scalar=0.5, in1=gz[:, :, :],
                                       op0=ALU.is_gt, op1=ALU.mult).then_inc(S["gw_ready"], 1)
                dve.wait_ge(S["gw_ready"], b + 1)
                if isinstance(b, int) and b == 0:
                    dve.wait_ge(S["hscale_ready"], 1)
                wait(dve, "gcur_ready", b)
                v.tensor_tensor(gsc[:, :, :], gw[:, :, :], dsc[0:P, :].unsqueeze(1).broadcast_to([P, NT, E]),
                                ALU.mult).then_inc(S["gsc_ready"], 1)
                dve.wait_ge(S["gwt_psum"], b + 1)
                v.tensor_copy(gwt, M[0:E, 1, 0:T]).then_inc(S["gwt_ready"], 1)
                dve.wait_ge(S["b2_psum"], b + 1)
                for j0, w in ((0, 2), (2, 1)):
                    src = M[0:P, 2 + j0 // 2, 0:w * D].rearrange("p (j c) -> p j c", j=w)
                    last = v.tensor_tensor(h0[:, j0:j0 + w, :], src, h0[:, j0:j0 + w, :], ALU.add)
                last.then_inc(S["base_ready"], 1)
                dve.wait_ge(S["x2hi_ready"], b + 1)
                v.tensor_tensor(x2[1], xT2[:, :, :], x2[0], ALU.subtract).then_inc(S["x2lo_ready"], 1)
                per_batch["steps"] = count[0]

            dve.wait_ge(S["ident_ready"], 1)
            for r in range(3):
                last = v.tensor_copy(pick[32 * r:32 * (r + 1), :], ident[32 * r:32 * (r + 1), 32 * r:32 * (r + 1)])
            v.memset(decay[:, :, :, :].rearrange("p a h t -> p (a h) t")[:, :, 0:1], 0.0).then_inc(S["a_cleared"], 1)
            v.memset(up0[:, :, 0:KC - 1], 0.0).then_inc(S["pad_zeroed"], 1)
            first_norm(0)
            dve.wait_ge(S["beta_psum"], 1)
            v.tensor_copy(tokb_s, M[0:1, 0, 0:D]).then_inc(S["tokb_ready"], 1)
            v.tensor_tensor(tokw_s[:, :, :], tokw_s[:, :, :], gam_s.unsqueeze(2).broadcast_to([128, FK, D]),
                            ALU.mult).then_inc(S["tokw_ready"], 1)
            first_norm(1)
            dve.wait_ge(S["whi_ready"], 1)
            hi, lo = [w[:, 0, :, :].rearrange("p a b -> p (a b)") for w in w1p]
            v.scalar_tensor_tensor(out=lo, in0=raw[SLOT[0]], scalar=s_w[:, 0, 0:1], in1=hi,
                                   op0=ALU.mult, op1=ALU.subtract).then_inc(S["wlo_first"], 1)
            dve.wait_ge(S["b1sq_ready"], 1)
            v.tensor_reduce(ssq[:, 2, :], hb_s[:, :, :], AX.X, ALU.add).then_inc(S["ab_done"], 1)
            batch(0, True)
            with dve.Fori(1, NB - 1) as i:
                batch(i, True)
            batch(NB - 1, False)

        @block.gpsimd
        def _(pool):
            g = nc.gpsimd
            nstep = [0]

            def step(ins):
                nstep[0] += 1
                ins.then_inc(S["pool_step"], 1)
                pool.wait_ge(S["pool_step"], nstep[0])

            def ahead_power(b, j, which):
                pool.wait_ge(S["hvar_ready" if which else "xvar_ready"], NT * b + j + 1)
                g.tensor_tensor(rsn[:, which:which + 1], ven[:, which:which + 1], nhalf[:, 0:1],
                                ALU.pow).then_inc(S["hrstd_ready" if which else "xrstd_ready"], 1)

            def power(b):
                pool.wait_ge(S["var_ready"], b + 1)
                g.tensor_tensor(rs[:, :], ve[:, :], nhalf[:, :], ALU.pow).then_inc(S["rstd_ready"], 1)

            def mixer(b, s, more):
                for p in range(NP):
                    for j in range(NT):
                        for which in range(2):
                            if more and s == at_pair(p) + 2 and p == norm_at(j, which):
                                ahead_power(b + 1, j, which)
                    if s == at_pair(p) + 3 and p > 0:
                        pool.wait_ge(S["part_ready"], NP * b + p + 1)
                        if p > 1:
                            pool.wait_ge(S["y_added"], (NP - 1) * b + p - 1)
                        g.tensor_tensor(y[:, :, :], y[:, :, :], part, ALU.add).then_inc(S["y_added"], 1)
                if s == AT_T2 - 2:
                    power(b)

            def low(f, s):
                pool.wait_ge(S["relu_done"], STEPS * f + s + 1 + ZR)
                g.tensor_tensor(hp[1][:, s % HR, 0:T], h32[:, s % HR, :], hp[0][:, s % HR, 0:T],
                                ALU.subtract).then_inc(S["lo_done"], 1)

            def gather(f, e):
                for t in range(NT):
                    pool.wait_ge(S["evac_done"], NT * (E * f + e) + t + 2)
                    if e > 0:
                        pool.wait_ge(S["acc_done"], NT * (E * f + e) + t + 1)
                    elif t == 0:
                        pool.wait_ge(S["acc_init"], f + 1)
                    g.tensor_tensor(acc[:, t, :], acc[:, t, :], tmp[:, t, :],
                                    ALU.add).then_inc(S["acc_done"], 1)

            def experts(f, s):
                low(f, s)
                if s == 4:
                    pool.wait_ge(S["out_done"], 16 * f + 16)
                    pool.wait_ge(S["base_ready"], f + 1)
                    pool.sem_inc(S["pool_passed"], 1)
                    g.tensor_copy(acc, h0[:, :, :]).then_inc(S["acc_init"], 1)
                if s % HJ == LAG + 1 and s > HJ:
                    gather(f, s // HJ - 1)

            def weight_scale(t):
                e, kind = TENSORS[t]
                one = lambda z, k: z[:, k, e:e + 1]
                pool.wait_ge(S["sq_done"], t + 1)
                step(g.partition_all_reduce(one(ssr, kind), one(ssq, kind), 128, RADD))
                step(g.tensor_scalar(one(ssr, kind), one(ssr, kind), WCAP ** -2, 1e-30, ALU.mult, ALU.add))
                step(g.tensor_tensor(one(i_w, kind), one(ssr, kind), exps[:, 1:2], ALU.pow))
                g.tensor_tensor(one(s_w, kind), one(ssr, kind), exps[:, 0:1], ALU.pow).then_inc(S["scale_done"], 1)

            def weight_low(t, half):
                e, kind = TENSORS[t]
                part_of = slice(half * 1024, half * 1024 + 1024)
                hi, lo = [w[:, e, :, :].rearrange("p a b -> p (a b)")[:, part_of] for w in (w1p if kind == 0 else w2p)]
                if half == 0:
                    pool.wait_ge(S["ws_ready"], t)
                g.tensor_tensor(lo, raw[SLOT[t]][:, part_of], hi, ALU.subtract).then_inc(S["wlo_done"], 1)

            def hidden_scales():
                step(g.partition_all_reduce(ssr[:, 2, :], ssq[:, 2, :], 128, RADD))
                step(g.tensor_scalar(ssr[:, 2, :], ssr[:, 2, :], WCAP ** -2, 1e-30, ALU.mult, ALU.add))
                step(g.tensor_tensor(fb[:, :], ssr[:, 2, :], exps[:, 1:2].broadcast_to([128, E]), ALU.pow))
                step(g.tensor_scalar(ih[:, :], i_w[:, 0, :], 16.0, 1.0, ALU.mult, ALU.mult))
                step(g.tensor_tensor(ih[:, :], ih[:, :], fb[:, :], ALU.add))
                step(g.tensor_tensor(sh[:, :], ih[:, :], exps[:, 2:3].broadcast_to([128, E]), ALU.pow))
                step(g.tensor_tensor(zs[:, :], sh[:, :], i_w[:, 0, :], ALU.mult))
                step(g.tensor_scalar(zs[:, :], zs[:, :], 1.0 / XS, 1.0, ALU.mult, ALU.mult))
                step(g.tensor_tensor(hb_s[:, :, :], b1_s[:, :, :], sh[:, :].unsqueeze(2).broadcast_to([128, E, HJ]),
                                     ALU.mult))
                g.tensor_tensor(dsc[:, :], ih[:, :], i_w[:, 1, :], ALU.mult).then_inc(S["hscale_ready"], 1)

            pool.sem_inc(S["lo_done"], HR)
            pool.sem_inc(S["acc_done"], NT)
            pool.sem_inc(S["out_done"], 16)
            g.memset(ident[:, :], 0.0).then_inc(S["ident_zero"], 1)
            g.memset(nhalf[:, :], -0.5)
            for n, value in enumerate((-0.5, 0.5, -1.0)):
                g.memset(exps[:, n:n + 1], value).then_inc(S["ident_set"], 1)
            pool.wait_ge(S["ident_zero"], 1)
            pool.wait_ge(S["ident_set"], 3)
            g.affine_select(out=ident[:, :], in_=ident[:, :], compare_op=ALU.not_equal, fill=1.0, base=0,
                            pattern=[[-1, 128]], channel_multiplier=1).then_inc(S["ident_ready"], 1)
            for kind in ("x", "h"):
                pool.wait_ge(S[kind + "var_ready"], NT)
                g.tensor_tensor(rs[:, :], ve[:, :], nhalf[:, :], ALU.pow).then_inc(S[kind + "rstd_ready"], NT)
            for t in range(2):
                weight_scale(t)
            pool.wait_ge(S["tok_in"], N_TOK)
            g.tensor_tensor(hb_s[:, :, :], b1_s[:, :, :], b1_s[:, :, :], ALU.mult).then_inc(S["b1sq_ready"], 1)
            for s in range(STEPS):
                mixer(0, s, True)
                for t in range(1, 2 * E):
                    if s == at_tensor(t) + TO_LOW[1]:
                        weight_low(t, 1)
                    if s == at_tensor(t) and t > 1:
                        weight_scale(t)
                    if s == at_tensor(t) + TO_LOW[0]:
                        weight_low(t, 0)
            pool.wait_ge(S["ab_done"], 1)
            hidden_scales()
            pool.wait_ge(S["wlo_done"], low_done(2 * E))
            for n in range(2):
                last = g.memset(hp[n][:, :, T:HW], 0.0)
            last.then_inc(S["hpad_zeroed"], 1)

            def both(b, more):
                for s in range(STEPS):
                    mixer(b, s, more)
                    experts(b - 1, s)
                gather(b - 1, E - 1)

            with pool.Fori(1, NB - 1) as i:
                both(i, True)
            both(NB - 1, False)
            for s in range(STEPS):
                experts(NB - 1, s)
            gather(NB - 1, E - 1)


def kernel(**inputs):
    import concourse.bacc as bacc
    from concourse.bass_utils import run_bass_kernel_spmd as run

    def arr(name):
        return np.asarray(inputs[name])

    def channels(a):
        return np.moveaxis(a.reshape(a.shape[0] // 128, 128, -1), 1, 0).reshape(128, -1)

    by_channel = [arr("L0_tok_ln_gamma"), arr("L0_tok_ln_beta"), arr("L0_attn_conv_w").reshape(D, KC),
                  arr("L0_attn_conv_b"), arr("L0_attn_A_log").T, arr("L0_attn_D_param"), arr("L0_ffn_Wg"),
                  arr("L0_ffn_b1").reshape(E * H)]
    given = {
        "x": arr("x"),
        "tok_w": arr("L0_tok_W").T,
        "tok_b": arr("L0_tok_b"),
        "chan": np.concatenate([channels(a) for a in by_channel], axis=1),
        "win": arr("L0_attn_W_in").T,
        "wout": arr("L0_attn_W_out").T,
        "bg": arr("L0_ffn_bg"),
        "w1": arr("L0_ffn_W1"),
        "w2": arr("L0_ffn_W2"),
        "b2": arr("L0_ffn_b2"),
    }
    nc = bacc.Bacc("TRN2", target_bir_lowering=False, num_devices=1)
    arrays, args = {}, []
    for name, a in given.items():
        a = np.ascontiguousarray(a)
        arrays[f"in_{name}"] = a
        args.append(nc.dram_tensor(f"in_{name}", a.shape, mybir.dt.from_np(a.dtype), kind="ExternalInput").ap())
    out = nc.dram_tensor("out_0", (NB, T, D), F32, kind="ExternalOutput").ap()
    build(nc, *args, out)
    r = run(nc, [arrays], core_ids=[0])
    return r.results[0]["out_0"]
```
